# Optimizing a Trainium2 kernel written in Bass

```python
import numpy as np
import jax
import jax.numpy as jnp

def _softmax(x, axis=-1):
    return jax.nn.softmax(x, axis=axis)

def _gelu(x):
    return jax.nn.gelu(x, approximate=True)

def _silu(x):
    return jax.nn.silu(x)

def _sigmoid(x):
    return jax.nn.sigmoid(x)

def _layernorm(x, axis=-1, eps=1e-05):
    m = jnp.mean(x, axis=axis, keepdims=True)
    v = jnp.var(x, axis=axis, keepdims=True)
    return (x - m) / jnp.sqrt(v + eps)

def _scatter_add(tgt, idx, src, axis=0):
    return tgt.at[idx].add(src)

def _segment_sum(src, seg, n):
    return jax.ops.segment_sum(src, seg, n)
kernel_name = 'mk_adj_ffn_d2_adj_r2_1c24be'

def setup_inputs(seed: int=0):
    np.random.seed(seed)
    _w = jnp.asarray

    def _rec_inputs():
        import jax
        import jax.numpy as jnp
        _gk = jax.random.key(seed)
        x = -0.0005207 + 1.001 * jax.random.normal(jax.random.fold_in(_gk, 1), (4096, 128), jnp.float32)
        _a = jax.random.bernoulli(jax.random.fold_in(_gk, 2), 0.000488281, (4096, 4096))
        _a = jnp.logical_or(_a, jnp.swapaxes(_a, -1, -2))
        _a = jnp.logical_or(_a, jnp.eye(4096, dtype=bool))
        _af = _a.astype(jnp.float32)
        _af = _af * jax.random.uniform(jax.random.fold_in(_gk, 3), (4096, 4096), jnp.float32, 0.05, 1)
        adj = _af
        return (x, adj)
    x, adj = _rec_inputs()

    def _L0_gnn_setup():
        import jax, jax.numpy as jnp
        import numpy as np
        THRESH = 1e-06
        EPS = 1e-08
        LN_EPS = 1e-05

        def _layer(h, M, W_in, b_in, W_out, b_out, W_self, b_self, gamma, beta):
            A = M / (jnp.sum(M, axis=0, keepdims=True) + EPS)
            mask = A > THRESH
            W = jnp.where(mask, A, 0.0)
            T = h @ W_in + b_in
            weighted_sum = jnp.einsum('ji,jd->id', W, T)
            weight_sum = jnp.sum(W, axis=0)
            has_edge = jnp.any(mask, axis=0)
            agg = jnp.where(has_edge[:, None], weighted_sum / (weight_sum[:, None] + EPS), T)
            agg = agg @ W_out + b_out
            out = agg + (h @ W_self + b_self)
            mu = jnp.mean(out, axis=-1, keepdims=True)
            var = jnp.mean(jnp.square(out - mu), axis=-1, keepdims=True)
            out = (out - mu) * jax.lax.rsqrt(var + LN_EPS) * gamma + beta
            return out
        key = jax.random.key(seed)
        ks = jax.random.split(key, 16)
        N, D_IN, D_H, D_OUT = (4096, 128, 256, 128)
        s = 0.05
        return {'node_features': jax.random.normal(ks[0], (N, D_IN), jnp.float32), 'mobility_matrix': jax.random.uniform(ks[1], (N, N), jnp.float32), 'W_in1': jax.random.normal(ks[2], (D_IN, D_H)) * s, 'b_in1': jnp.zeros((D_H,)), 'W_out1': jax.random.normal(ks[3], (D_H, D_H)) * s, 'b_out1': jnp.zeros((D_H,)), 'W_self1': jax.random.normal(ks[4], (D_IN, D_H)) * s, 'b_self1': jnp.zeros((D_H,)), 'g1': jnp.ones((D_H,)), 'be1': jnp.zeros((D_H,)), 'W_in2': jax.random.normal(ks[5], (D_H, D_OUT)) * s, 'b_in2': jnp.zeros((D_OUT,)), 'W_out2': jax.random.normal(ks[6], (D_OUT, D_OUT)) * s, 'b_out2': jnp.zeros((D_OUT,)), 'W_self2': jax.random.normal(ks[7], (D_H, D_OUT)) * s, 'b_self2': jnp.zeros((D_OUT,)), 'g2': jnp.ones((D_OUT,)), 'be2': jnp.zeros((D_OUT,))}
    _L0_gnn_all = _L0_gnn_setup()
    _L0_gnn_in = {k: v for k, v in _L0_gnn_all.items() if k in ('W_in1', 'b_in1', 'W_out1', 'b_out1', 'W_self1', 'b_self1', 'g1', 'be1', 'W_in2', 'b_in2', 'W_out2', 'b_out2', 'W_self2', 'b_self2', 'g2', 'be2')}
    del _L0_gnn_all

    def _L0_ffn_setup():
        import math
        import jax, jax.numpy as jnp
        import numpy as np
        CAPACITY_FACTOR = 1.25
        key = jax.random.key(seed)
        ks = jax.random.split(key, 5)
        B, L, D, F, E = (8, 4096, 128, 512, 8)
        h = jax.random.normal(ks[0], (B, L, D), dtype=jnp.float32)
        gate_w = jax.random.normal(ks[1], (D, E), dtype=jnp.float32) * 0.02
        gate_b = jnp.zeros((E,), dtype=jnp.float32)
        w1 = jax.random.normal(ks[2], (E, D, F), dtype=jnp.float32) * (1.0 / math.sqrt(D))
        b1 = jnp.zeros((E, F), dtype=jnp.float32)
        w2 = jax.random.normal(ks[3], (E, F, D), dtype=jnp.float32) * (1.0 / math.sqrt(F))
        b2 = jnp.zeros((E, D), dtype=jnp.float32)
        return {'h': h, 'gate_w': gate_w, 'gate_b': gate_b, 'w1': w1, 'b1': b1, 'w2': w2, 'b2': b2}
    _L0_ffn_all = _L0_ffn_setup()
    _L0_ffn_in = {k: v for k, v in _L0_ffn_all.items() if k in ('gate_w', 'gate_b', 'w1', 'b1', 'w2', 'b2')}
    del _L0_ffn_all

    def _L1_gnn_setup():
        import jax, jax.numpy as jnp
        import numpy as np
        N = 5000
        F = 128
        key = jax.random.key(seed)
        k1, k2 = jax.random.split(key)
        x = jax.random.normal(k1, (N, F), dtype=jnp.float32)
        A = jax.random.uniform(k2, (N, N), dtype=jnp.float32)
        W = jnp.ones((F,), dtype=jnp.float32)
        return {'input': x, 'A': A, 'W': W}
    _L1_gnn_all = _L1_gnn_setup()
    _L1_gnn_in = {k: v for k, v in _L1_gnn_all.items() if k in ('W',)}
    del _L1_gnn_all

    def _L1_ffn_setup():
        import jax, jax.numpy as jnp
        import numpy as np
        B, T, IN_DIM = (64, 128, 128)
        HID, OUT_DIM = (256, 128)
        N_LAYERS, N_EXPERTS, N_SHARED = (2, 16, 1)
        key = jax.random.key(seed)
        ks = jax.random.split(key, 10)
        s = 0.02
        x = jax.random.normal(ks[0], (B, T, IN_DIM), dtype=jnp.float32)
        route_id = jax.random.randint(ks[1], (B,), 0, N_EXPERTS)
        Wi = jax.random.normal(ks[2], (HID, IN_DIM), dtype=jnp.float32) * s
        bi = jnp.zeros((HID,), dtype=jnp.float32)
        Wr = jax.random.normal(ks[3], (N_LAYERS, N_EXPERTS, HID, HID), dtype=jnp.float32) * s
        br = jax.random.normal(ks[4], (N_LAYERS, N_EXPERTS, HID), dtype=jnp.float32) * s
        Ws = jax.random.normal(ks[5], (N_LAYERS, N_SHARED, HID, HID), dtype=jnp.float32) * s
        bs = jax.random.normal(ks[6], (N_LAYERS, N_SHARED, HID), dtype=jnp.float32) * s
        Wo = jax.random.normal(ks[7], (OUT_DIM, HID), dtype=jnp.float32) * s
        bo = jnp.zeros((OUT_DIM,), dtype=jnp.float32)
        return {'x': x, 'route_id': route_id, 'Wi': Wi, 'bi': bi, 'Wr': Wr, 'br': br, 'Ws': Ws, 'bs': bs, 'Wo': Wo, 'bo': bo}
    _L1_ffn_all = _L1_ffn_setup()
    _L1_ffn_in = {k: v for k, v in _L1_ffn_all.items() if k in ('route_id', 'Wi', 'bi', 'Wr', 'br', 'Ws', 'bs', 'Wo', 'bo')}
    del _L1_ffn_all
    return {'x': x, 'adj': adj, 'L0_gnn_W_in1': _L0_gnn_in['W_in1'], 'L0_gnn_b_in1': _L0_gnn_in['b_in1'], 'L0_gnn_W_out1': _L0_gnn_in['W_out1'], 'L0_gnn_b_out1': _L0_gnn_in['b_out1'], 'L0_gnn_W_self1': _L0_gnn_in['W_self1'], 'L0_gnn_b_self1': _L0_gnn_in['b_self1'], 'L0_gnn_g1': _L0_gnn_in['g1'], 'L0_gnn_be1': _L0_gnn_in['be1'], 'L0_gnn_W_in2': _L0_gnn_in['W_in2'], 'L0_gnn_b_in2': _L0_gnn_in['b_in2'], 'L0_gnn_W_out2': _L0_gnn_in['W_out2'], 'L0_gnn_b_out2': _L0_gnn_in['b_out2'], 'L0_gnn_W_self2': _L0_gnn_in['W_self2'], 'L0_gnn_b_self2': _L0_gnn_in['b_self2'], 'L0_gnn_g2': _L0_gnn_in['g2'], 'L0_gnn_be2': _L0_gnn_in['be2'], 'L0_ffn_gate_w': _L0_ffn_in['gate_w'], 'L0_ffn_gate_b': _L0_ffn_in['gate_b'], 'L0_ffn_w1': _L0_ffn_in['w1'], 'L0_ffn_b1': _L0_ffn_in['b1'], 'L0_ffn_w2': _L0_ffn_in['w2'], 'L0_ffn_b2': _L0_ffn_in['b2'], 'L1_gnn_W': _L1_gnn_in['W'], 'L1_ffn_route_id': _L1_ffn_in['route_id'], 'L1_ffn_Wi': _L1_ffn_in['Wi'], 'L1_ffn_bi': _L1_ffn_in['bi'], 'L1_ffn_Wr': _L1_ffn_in['Wr'], 'L1_ffn_br': _L1_ffn_in['br'], 'L1_ffn_Ws': _L1_ffn_in['Ws'], 'L1_ffn_bs': _L1_ffn_in['bs'], 'L1_ffn_Wo': _L1_ffn_in['Wo'], 'L1_ffn_bo': _L1_ffn_in['bo']}

def reference(x, adj, L0_gnn_W_in1, L0_gnn_b_in1, L0_gnn_W_out1, L0_gnn_b_out1, L0_gnn_W_self1, L0_gnn_b_self1, L0_gnn_g1, L0_gnn_be1, L0_gnn_W_in2, L0_gnn_b_in2, L0_gnn_W_out2, L0_gnn_b_out2, L0_gnn_W_self2, L0_gnn_b_self2, L0_gnn_g2, L0_gnn_be2, L0_ffn_gate_w, L0_ffn_gate_b, L0_ffn_w1, L0_ffn_b1, L0_ffn_w2, L0_ffn_b2, L1_gnn_W, L1_ffn_route_id, L1_ffn_Wi, L1_ffn_bi, L1_ffn_Wr, L1_ffn_br, L1_ffn_Ws, L1_ffn_bs, L1_ffn_Wo, L1_ffn_bo):
    import jax
    import jax.numpy as jnp

    def _L0_gnn_ref(node_features, mobility_matrix, W_in1, b_in1, W_out1, b_out1, W_self1, b_self1, g1, be1, W_in2, b_in2, W_out2, b_out2, W_self2, b_self2, g2, be2):
        import jax, jax.numpy as jnp
        import numpy as np
        THRESH = 1e-06
        EPS = 1e-08
        LN_EPS = 1e-05

        def _layer(h, M, W_in, b_in, W_out, b_out, W_self, b_self, gamma, beta):
            A = M / (jnp.sum(M, axis=0, keepdims=True) + EPS)
            mask = A > THRESH
            W = jnp.where(mask, A, 0.0)
            T = h @ W_in + b_in
            weighted_sum = jnp.einsum('ji,jd->id', W, T)
            weight_sum = jnp.sum(W, axis=0)
            has_edge = jnp.any(mask, axis=0)
            agg = jnp.where(has_edge[:, None], weighted_sum / (weight_sum[:, None] + EPS), T)
            agg = agg @ W_out + b_out
            out = agg + (h @ W_self + b_self)
            mu = jnp.mean(out, axis=-1, keepdims=True)
            var = jnp.mean(jnp.square(out - mu), axis=-1, keepdims=True)
            out = (out - mu) * jax.lax.rsqrt(var + LN_EPS) * gamma + beta
            return out
        h = _layer(node_features, mobility_matrix, W_in1, b_in1, W_out1, b_out1, W_self1, b_self1, g1, be1)
        h = jax.nn.relu(h)
        h = _layer(h, mobility_matrix, W_in2, b_in2, W_out2, b_out2, W_self2, b_self2, g2, be2)
        h = jax.nn.relu(h)
        return h

    def _L0_ffn_ref(h, gate_w, gate_b, w1, b1, w2, b2):
        import math
        import jax, jax.numpy as jnp
        import numpy as np
        CAPACITY_FACTOR = 1.25
        B, L, D = h.shape
        E = gate_w.shape[1]
        T = B * L
        C = max(1, math.ceil(CAPACITY_FACTOR * T / E))
        x = h.reshape(T, D)
        logits = x @ gate_w + gate_b
        probs = jax.nn.softmax(logits, axis=-1)
        idx = jnp.argmax(probs, axis=-1)
        prb = jnp.take_along_axis(probs, idx[:, None], axis=1)[:, 0]
        one_hot = jax.nn.one_hot(idx, E, dtype=jnp.float32)
        pos = (jnp.cumsum(one_hot, axis=0) * one_hot).sum(-1).astype(jnp.int32) - 1
        kept = pos < C
        pos_safe = jnp.where(kept, pos, C)
        buf = jnp.zeros((E, C, D), dtype=h.dtype).at[idx, pos_safe].set(x, mode='drop')
        hmid = jax.nn.relu(jnp.einsum('ecd,edf->ecf', buf, w1) + b1[:, None, :])
        ybuf = jnp.einsum('ecf,efd->ecd', hmid, w2) + b2[:, None, :]
        pos_g = jnp.minimum(pos, C - 1)
        y_tok = ybuf[idx, pos_g] * (prb * kept)[:, None]
        y = y_tok.reshape(B, L, D)
        y = jnp.nan_to_num(y, nan=0.0, posinf=10000.0, neginf=-10000.0)
        return y

    def _L1_gnn_ref(input, A, W):
        import jax, jax.numpy as jnp
        import numpy as np
        N = 5000
        F = 128
        hidden = input * W
        return A @ hidden

    def _L1_ffn_ref(x, route_id, Wi, bi, Wr, br, Ws, bs, Wo, bo):
        import jax, jax.numpy as jnp
        import numpy as np
        B, T, IN_DIM = (64, 128, 128)
        HID, OUT_DIM = (256, 128)
        N_LAYERS, N_EXPERTS, N_SHARED = (2, 16, 1)
        flat = x.reshape(-1, x.shape[-1])
        n_tok = flat.shape[0]
        route = jnp.repeat(route_id, n_tok // route_id.shape[0])
        h = jax.nn.relu(flat @ Wi.T + bi)
        n_layers, n_experts = (Wr.shape[0], Wr.shape[1])
        for l in range(n_layers):
            shared = (jnp.einsum('nd,shd->snh', h, Ws[l]) + bs[l][:, None, :]).mean(axis=0)
            routed = jnp.zeros_like(h)
            for e in range(n_experts):
                ye = h @ Wr[l, e].T + br[l, e]
                routed = routed + jnp.where((route == e)[:, None], ye, 0.0)
            h = jax.nn.relu(shared + routed + h)
        out = h @ Wo.T + bo
        return out.reshape(*x.shape[:-1], out.shape[-1])
    x = x + _L0_gnn_ref(_layernorm(x, axis=-1), adj, L0_gnn_W_in1, L0_gnn_b_in1, L0_gnn_W_out1, L0_gnn_b_out1, L0_gnn_W_self1, L0_gnn_b_self1, L0_gnn_g1, L0_gnn_be1, L0_gnn_W_in2, L0_gnn_b_in2, L0_gnn_W_out2, L0_gnn_b_out2, L0_gnn_W_self2, L0_gnn_b_self2, L0_gnn_g2, L0_gnn_be2)
    x = x + _L0_ffn_ref(_layernorm(x, axis=-1)[None], L0_ffn_gate_w, L0_ffn_gate_b, L0_ffn_w1, L0_ffn_b1, L0_ffn_w2, L0_ffn_b2)[0]
    x = x + _L1_gnn_ref(_layernorm(x, axis=-1), adj, L1_gnn_W)
    x = x + _L1_ffn_ref(_layernorm(x, axis=-1)[None], L1_ffn_route_id, L1_ffn_Wi, L1_ffn_bi, L1_ffn_Wr, L1_ffn_br, L1_ffn_Ws, L1_ffn_bs, L1_ffn_Wo, L1_ffn_bo)[0]
    return x

_drawn_inputs = setup_inputs


def setup_inputs(seed=0):
    import zlib

    import numpy as np

    out = dict(_drawn_inputs(seed))
    spreads = {'L0_gnn_b_in1': (0.0, 0.1),
     'L0_gnn_b_out1': (0.0, 0.1),
     'L0_gnn_b_self1': (0.0, 0.1),
     'L0_gnn_g1': (1.0, 0.2),
     'L0_gnn_be1': (0.0, 0.1),
     'L0_gnn_b_in2': (0.0, 0.1),
     'L0_gnn_b_out2': (0.0, 0.1),
     'L0_gnn_b_self2': (0.0, 0.1),
     'L0_gnn_g2': (1.0, 0.2),
     'L0_gnn_be2': (0.0, 0.1),
     'L0_ffn_gate_b': (0.0, 0.1),
     'L0_ffn_b1': (0.0, 0.8),
     'L0_ffn_b2': (0.0, 0.711),
     'L1_gnn_W': (1.0, 0.2),
     'L1_ffn_bi': (0.0, 0.8),
     'L1_ffn_bo': (0.0, 0.1)}
    factors = {'L1_ffn_Wi': 3.341,
     'L1_ffn_Wr': 7.205,
     'L1_ffn_br': 8.0,
     'L1_ffn_Ws': 7.185,
     'L1_ffn_bs': 8.0}
    for name, (base, spread) in spreads.items():
        noise = np.random.default_rng([zlib.crc32(name.encode()), seed]).standard_normal(out[name].shape)
        drawn = base * np.exp(spread * noise) if base else spread * noise
        out[name] = jnp.asarray(drawn.astype(out[name].dtype))
    for name, factor in factors.items():
        out[name] = (out[name] * factor).astype(out[name].dtype)
    return out
```

```python
from contextlib import ExitStack

import concourse.bass as bass
from concourse import mybir

F32 = mybir.dt.float32
BF16 = mybir.dt.bfloat16
I8 = mybir.dt.int8
I32 = mybir.dt.int32
U32 = mybir.dt.uint32
ALU = mybir.AluOpType
ACT = mybir.ActivationFunctionType
AX = mybir.AxisListType
ds = bass.ds

P = 128
N = 4096
D = 128
DH = 256
NT = N // P
BT = 4
BW = BT * P
NB = N // BW
HT = NT // 2
HALF = HT * BW
QT = NT // 4
QUART = QT * BW
E1 = 8
F1 = 512
FK = F1 // P
CAP = -(-5 * N // (4 * E1))
CT = CAP // P
ROW = D + 2
E2 = 16
SEG = N // 64
SB = BW // SEG
KH = DH // P
L2 = 2
SH = SB // 2
NG = L2 * SB // SH

THRESH = 1e-6
EPS = 1e-8
LN_EPS = 1e-5
SMALL = 2.0 ** -6
FMAX = 3.4028234e38
BIG = 1.0e4
NOWHERE = 1.0e6
CW = 2048
NC = HALF // CW


def build(nc, A, out):
    ctx = ExitStack()
    with ctx:
        def sb(name, shape, dt=F32):
            return ctx.enter_context(nc.sbuf_tensor(name, shape, dt))

        def pb(name, shape, dt=F32):
            return ctx.enter_context(nc.psum_tensor(name, shape, dt))

        def sem(name):
            return ctx.enter_context(nc.semaphore(name))

        thr_d = nc.dram_tensor("thr_d", [NB, BW], F32).ap()
        disp_d = nc.dram_tensor("disp_d", [E1 * CAP, ROW], F32).ap()
        y_d = nc.dram_tensor("y_d", [N, D], F32).ap()

        ring = [[sb(f"ring{s}{h}", [P, HALF]) for h in range(2)] for s in range(2)]
        S = sb("S", [P, NT * D])
        U = sb("U", [P, NT * D])
        R = sb("R", [P, NT * D])

        ident = sb("ident", [P, P])
        ones = sb("ones", [P, P])
        onesb = sb("onesb", [P, P], BF16)
        tri = sb("tri", [P, P], BF16)
        W_io = sb("W_io", [P, DH])
        W_s1 = sb("W_s1", [P, DH])
        W_us = sb("W_us", [P, KH, 2 * D])
        b_io = sb("b_io", [P, DH])
        b_all = sb("b_all", [P, DH])
        b_us = sb("b_us", [P, 2 * D])
        gb1 = sb("gb1", [P, 2 * KH])
        wgate = sb("wgate", [P, E1])
        rb = sb("rb", [P, NT])
        ne = sb("ne", [P, NT])
        neg_half = sb("neg_half", [P, 8])
        flags = sb("flags", [1, NB], I32)
        small = sb("small", [P, 96])
        sumc, rbp, cc, rs_, ws_, rw_, nn = [small[:, 4 * i:4 * i + 4] for i in range(7)]
        smax, cdiff, bad1, bad = [small[:, 28 + i:29 + i] for i in range(4)]
        ve = small[:, 32:40]
        rstd = small[:, 40:48]
        csum = small[:, 48:48 + 2 * NC]
        cshift = small[:, 56:56 + 2 * NC]
        st6 = sb("st6", [P, 8 * 6])
        mv = sb("mv", [P, 8 * 2])
        WORK = 22 * 256 + 64
        work = sb("work", [P, WORK])

        def part(at, n):
            return work[:, at:at + n]

        pA, thr, aT, hT, hs = [part(BW * i, BW) for i in range(5)]
        pre = [part(5 * BW + DH * i, DH) for i in range(2)]
        z1 = part(6 * BW, BT * DH)
        h1T = part(8 * BW, KH * BW)
        junk = part(10 * BW, CW // 4).bitcast(I8)
        p2T, xb, o2, hnT, msk = [part(BW * i, BW) for i in range(5)]
        thr2 = [part(BW * (5 + i), BW) for i in range(2)]
        rows = part(7 * BW, BT * ROW)
        at = 7 * BW + BT * ROW
        g2, be2 = part(at, D), part(at + D, D)
        at += 2 * D
        lg, ex, sc, cw, w8, cofs, gbc = [part(at + 32 * i, 32) for i in range(7)]
        at += 224
        lmax, esum, slot, tok, tok0 = [part(at + 4 * i, 4) for i in range(5)]
        at += 20
        off = part(at, 5 * E1)
        at += 5 * E1
        idx = part(at, BT).bitcast(U32)
        at += 4
        oh = part(at, 16).bitcast(BF16)
        at += 16
        rb4, ne4 = part(at, 4), part(at + 4, 4)
        assert at + 8 <= WORK

        at = 0
        e_rows = [part(at + CT * ROW * i, CT * ROW) for i in range(2)]
        at += 2 * CT * ROW
        e_w1 = [part(at + F1 * i, F1) for i in range(2)]
        at += 2 * F1
        e_w2 = [part(at + F1 * i, FK * D) for i in range(2)]
        at += 2 * FK * D
        e_b2 = [part(at + D * i, D) for i in range(2)]
        at += 2 * D
        e_b1 = [part(at + FK * i, FK) for i in range(2)]
        at += 2 * FK
        e_idx = [part(at + 8 * i, CT).bitcast(U32) for i in range(2)]
        at += 16
        e_xT = U[:, 0:CAP]
        e_hm = U[:, CAP:(1 + FK) * CAP]
        e_y = [R[:, CAP * i:CAP * (i + 1)] for i in range(2)]
        e_fin, e_pos, e_neg = [R[:, CAP * (2 + i):CAP * (3 + i)] for i in range(3)]
        w_i = part(at, DH)
        at += DH
        w_s = part(at, L2 * KH * DH)
        at += L2 * KH * DH
        w_o = part(at, KH * D)
        at += KH * D
        b_o = part(at, D)
        at += D
        b_i = part(at, KH)
        b_r = part(at + KH, L2 * KH * E2)
        at += KH + L2 * KH * E2
        b_s = part(at, L2 * KH)
        w_g = part(at + L2 * KH, 1)
        at += L2 * KH + 1
        route_sb = part(at, N // SEG)[0:1].bitcast(I32)
        assert at + N // SEG <= WORK
        F2_INPUTS = [(w_i, "WiT"), (w_s, "WsT"), (w_o, "WoT"), (b_o, "bo_bc"), (b_i, "bi"), (b_r, "br"), (b_s, "bs"),
                     (w_g, "gnn_W"), (route_sb[:, :], "route")]
        oT, x3, hn3, hT3, ob = [part(BW * i, BW) for i in range(5)]
        h_b = part(5 * BW, KH * BW)
        assert 7 * BW <= 2 * CT * ROW + 2 * F1 + 2 * FK * D + 2 * D + 2 * FK + 16
        h_a = U[:, 0:KH * BW]
        WS = 4
        wst = [U[:, KH * BW + KH * DH * i:KH * BW + KH * DH * (i + 1)] for i in range(WS)]

        def tiles(ap, n=BT, w=D):
            return ap.rearrange("p (t d) -> p t d", t=n, d=w)

        fill = R[:, 0:10 * ROW]
        t_at = 1408
        t_in1T = R[:, t_at:t_at + 256]
        t_out1 = R[:, t_at + 256:t_at + 768]
        t_in2T = R[:, t_at + 768:t_at + 1024]
        t_out2 = R[:, t_at + 1024:t_at + 1152]
        t_bin1 = R[:, t_at + 1152:t_at + 1408]
        t_bin2 = R[:, t_at + 1408:t_at + 1536]
        t_bs1 = R[:, t_at + 1536:t_at + 1792]
        t_bs2 = R[:, t_at + 1792:t_at + 1920]

        PA = [pb(f"PA{i}", [P, BW]) for i in range(2)]
        SR = pb("SR", [P, BW])
        SM = pb("SM", [P, BW])
        T = [pb(f"T{i}", [P, BW]) for i in range(2)]
        O = [pb(f"O{i}", [P, BW]) for i in range(2)]
        HB = [PA[0], PA[1], SR, SM]
        LB = [SR, SM, O[0], O[1]]

        s_wts = sem("s_wts")
        s_wts2 = sem("s_wts2")
        s_xin = [sem(f"s_xin{c}") for c in range(4)]
        s_ring = [[sem(f"s_ring{s}{q}") for q in range(4)] for s in range(2)]
        s_const = sem("s_const")
        s_zero = sem("s_zero")
        s_fill = sem("s_fill")
        s_wprod = sem("s_wprod")
        s_wready = sem("s_wready")
        s_mv0 = sem("s_mv0")
        s_rstd0 = sem("s_rstd0")
        s_hn = sem("s_hn")
        s_ms = sem("s_ms")
        s_msp = sem("s_msp")
        s_part = sem("s_part")
        s_sums = sem("s_sums")
        s_thr = sem("s_thr")
        s_thrst = sem("s_thrst")
        s_cnt = sem("s_cnt")
        s_bad = sem("s_bad")
        s_flag = sem("s_flag")
        s_clean = sem("s_clean")
        s_quart = sem("s_quart")
        s_agg = sem("s_agg")
        s_aT = sem("s_aT")
        s_neh = sem("s_neh")
        s_hs = sem("s_hs")
        s_hTp = sem("s_hTp")
        s_hT = sem("s_hT")
        s_o1 = sem("s_o1")
        s_o1u = sem("s_o1u")
        s_pre = sem("s_pre")
        s_mv = sem("s_mv")
        s_rstd = sem("s_rstd")
        s_z = sem("s_z")
        s_zT = sem("s_zT")
        s_h1T = sem("s_h1T")
        s_u2 = sem("s_u2")
        s_u2u = sem("s_u2u")
        s_thr2 = [sem(f"s_thr2{i}") for i in range(2)]
        s_clean2 = sem("s_clean2")
        s_quart2 = sem("s_quart2")
        s_agg2 = sem("s_agg2")
        s_p2 = sem("s_p2")
        s_t2 = sem("s_t2")
        s_t2u = sem("s_t2u")
        s_mv2 = sem("s_mv2")
        s_rstd2 = sem("s_rstd2")
        s_xb = sem("s_xb")
        s_x1 = sem("s_x1")
        s_hn2 = sem("s_hn2")
        s_hn2p = sem("s_hn2p")
        s_hn2T = sem("s_hn2T")
        s_lg = sem("s_lg")
        s_l2 = sem("s_l2")
        s_ex = sem("s_ex")
        s_oh = sem("s_oh")
        s_cum = sem("s_cum")
        s_idx = sem("s_idx")
        s_sc = sem("s_sc")
        s_ein = [sem(f"s_ein{i}") for i in range(2)]
        s_xTp = sem("s_xTp")
        s_xT = sem("s_xT")
        s_h1 = sem("s_h1")
        s_hm = sem("s_hm")
        s_yp = sem("s_yp")
        s_ye = sem("s_ye")
        s_y = sem("s_y")
        s_sc2 = [sem(f"s_sc2{i}") for i in range(2)]
        s_wts3 = sem("s_wts3")
        s_yin = [sem(f"s_yin{c}") for c in range(4)]
        s_mv3 = sem("s_mv3")
        s_rstd3 = sem("s_rstd3")
        s_hid = sem("s_hid")
        s_quart3 = sem("s_quart3")
        s_agg3 = sem("s_agg3")
        s_oT = sem("s_oT")
        s_oTt = sem("s_oTt")
        s_x3 = sem("s_x3")
        s_mv4 = sem("s_mv4")
        s_rstd4 = sem("s_rstd4")
        s_hn3 = sem("s_hn3")
        s_hn3p = sem("s_hn3p")
        s_hT3 = sem("s_hT3")
        s_h0p = sem("s_h0p")
        s_h0 = sem("s_h0")
        s_wst = sem("s_wst")
        s_wu = sem("s_wu")
        s_l = sem("s_l")
        s_fin = sem("s_fin")
        s_x3b = sem("s_x3b")
        s_out = sem("s_out")
        s_stored = sem("s_stored")
        s_fin2 = sem("s_fin2")

        def load_quarter(eng, M, b, slot, q):
            at = q % 2 * QUART
            eng.dma_start(ring[slot][q // 2][:, at:at + QUART],
                          M[ds(b, 1), :, q * QUART:(q + 1) * QUART].rearrange("o p n -> (o p) n")).then_inc(s_ring[slot][q], 16)

        def peeled(eng, step, drain):
            step(0, 0, 0, False, True)
            with eng.Fori(0, NB // 2 - 1) as i:
                step(i * 2 + 1, 1, i, True, True)
                step(i * 2 + 2, 0, i + 1, True, True)
            step(NB - 1, 1, NB // 2 - 1, True, False)
            drain(NB)

        def scan(eng, k):
            return (NB - 1) - k

        ticks = {nc.sync: sem("tick_sp"), nc.scalar: sem("tick_act"), nc.gpsimd: sem("tick_pool"), nc.vector: sem("tick_dve")}

        def alone(eng):
            eng.sem_inc(ticks[eng], 1)


        adjc, adjT = A["adj_cols"], A["adjT_cols"]
        x_t = A["x"].rearrange("(t p) d -> p t d", p=P)
        disp_t = disp_d.rearrange("(t p) r -> p t r", p=P)
        y_t = y_d.rearrange("(t p) d -> p t d", p=P)
        out_t = out.rearrange("(t p) d -> p t d", p=P)
        block = ctx.enter_context(nc.Block())

        @block.sync
        def _(sp):
            for c in range(4):
                sp.dma_start(tiles(S[:, c * 1024:(c + 1) * 1024], 8), x_t[:, 8 * c:8 * c + 8, :]).then_inc(s_xin[c], 16)
            for k in range(2):
                for q in range(4):
                    load_quarter(sp, adjc, scan(sp, k), k, q)
                if k == 0:
                    sp.wait_ge(s_zero, 1)
                    sp.dma_start(y_d.rearrange("(p t) d -> p (t d)", p=P), U[:, :]).then_inc(s_fill, 16)
                    for q in range(4):
                        n = E1 * CAP // 4
                        sp.dma_start(disp_d[q * n:(q + 1) * n, :].rearrange("(p t) r -> p (t r)", p=P), fill).then_inc(s_fill, 16)

            def store_thr(k):
                sp.wait_ge(s_thr, k + 1)
                alone(sp)
                sp.dma_start(thr_d[ds(scan(sp, k), 1), :], thr[0:1, :]).then_inc(s_thrst, 16)

            def refill(k, slot):
                for q in range(3):
                    sp.wait_ge(s_quart, (k - 2) * 3 + q + 1)
                    alone(sp)
                    load_quarter(sp, adjc, scan(sp, k), slot, q)
                store_thr(k - 1)
                sp.wait_ge(s_agg, k - 1)
                alone(sp)
                load_quarter(sp, adjc, scan(sp, k), slot, 3)

            store_thr(0)
            with sp.Fori(0, NB // 2 - 1) as i:
                refill(i * 2 + 2, 0)
                refill(i * 2 + 3, 1)
            store_thr(NB - 1)
            sp.wait_ge(s_thrst, 16 * NB)

            def block_inputs(j, slot, first):
                if not first:
                    sp.wait_ge(s_clean2, j - 1)
                    alone(sp)
                sp.dma_start(thr2[slot][:, :], thr_d[ds(j, 1), :].to_broadcast([P, BW])).then_inc(s_thr2[slot], 16)

            def load_xb(j):
                sp.wait_ge(s_x1, j + 1)
                alone(sp)
                sp.dma_start(tiles(xb), x_t[:, ds(j * BT, BT), :]).then_inc(s_xb, 16)

            sp.wait_ge(s_u2u, 2 + 2 * NB)
            sp.dma_start(g2, A["g2_bc"]).then_inc(s_wts2, 16)
            sp.dma_start(be2, A["be2_bc"]).then_inc(s_wts2, 16)
            sp.dma_start(gbc, A["gate_b_bc"]).then_inc(s_wts2, 16)
            block_inputs(0, 1, True)
            block_inputs(1, 0, True)

            def refill2(j, slot):
                for q in range(4):
                    if q < 3:
                        sp.wait_ge(s_quart2, (j - 2) * 3 + q + 1)
                    else:
                        sp.wait_ge(s_agg2, j - 1)
                    alone(sp)
                    load_quarter(sp, adjc, j, slot, q)
                    if q == 1:
                        load_xb(j - 2)
                block_inputs(j, slot, False)

            with sp.Fori(0, NB // 2 - 1) as i:
                refill2(i * 2 + 2, 1)
                refill2(i * 2 + 3, 0)
            load_xb(NB - 2)

            for q in range(4):
                if q < 3:
                    sp.wait_ge(s_quart2, (NB - 2) * 3 + q + 1)
                else:
                    sp.wait_ge(s_agg2, NB - 1)
                load_quarter(sp, adjT, 0, 1, q)
            load_xb(NB - 1)
            sp.wait_ge(s_sc, 16 * NT)

            def load_expert(e, par):
                sp.wait_ge(s_y, e + 1)
                alone(sp)
                sp.dma_start(tiles(e_rows[par], CT, ROW), disp_t[:, ds(e * CT, CT), :]).then_inc(s_ein[par], 16)
                sp.dma_start(e_w1[par], A["w1"][ds(e, 1)].rearrange("o p f -> (o p) f")).then_inc(s_ein[par], 16)
                sp.dma_start(e_w2[par], A["w2"][ds(e, 1)].rearrange("o p f -> (o p) f")).then_inc(s_ein[par], 16)
                sp.dma_start(e_b1[par], A["b1"][ds(e, 1)].rearrange("o p f -> (o p) f")).then_inc(s_ein[par], 16)
                sp.dma_start(e_b2[par], A["b2_bc"][ds(e, 1)].rearrange("o p f -> (o p) f")).then_inc(s_ein[par], 16)

            load_expert(0, 0)
            load_expert(1, 1)
            sp.wait_ge(s_agg2, NB)
            for dst, name in F2_INPUTS:
                sp.dma_start(dst, A[name]).then_inc(s_wts3, 16)
            for l in range(L2):
                sp.dma_start(ring[0][l][:, :], A["Wr"][l]).then_inc(s_ring[0][2 * l], 16)
            with sp.Fori(1, E1 // 2) as i:
                load_expert(i * 2, 0)
                load_expert(i * 2 + 1, 1)

            for par in range(2):
                sp.wait_ge(s_sc2[par], 16 * CT * E1 // 2)
            for c in range(4):
                sp.dma_start(tiles(R[:, c * 1024:(c + 1) * 1024], 8), y_t[:, 8 * c:8 * c + 8, :]).then_inc(s_yin[c], 16)

            with sp.Fori(1, NB) as b:
                for q in range(4):
                    if q < 3:
                        sp.wait_ge(s_quart3, (b - 1) * 3 + q + 1)
                    else:
                        sp.wait_ge(s_agg3, b)
                    alone(sp)
                    load_quarter(sp, adjT, b, 1, q)
            sp.wait_ge(s_stored, 16 * NB)

        @block.scalar
        def _(act):
            for dst, name in ((t_in1T, "W_in1T"), (t_out1, "W_out1"), (t_in2T, "W_in2T"), (t_out2, "W_out2"),
                              (t_bin1, "b_in1_rep"), (t_bin2, "b_in2_rep"), (t_bs1, "b_self1_bc"), (t_bs2, "b_self2_bc"),
                              (b_all[:, :], "b_out1_bc"), (b_us[:, D:2 * D], "b_out2_bc"), (W_s1[:, :], "W_self1"),
                              (W_us[:, :, D:2 * D], "W_self2"), (gb1[:, :], "gb1"), (wgate[:, :], "gate_w")):
                act.dma_start(dst, A[name]).then_inc(s_wts, 16)

            def check(k, slot, rnd):
                act.wait_ge(s_bad, k + 1)
                alone(act)
                for col in range(2 * NC):
                    if col % (NC // 2) == 0:
                        act.wait_ge(s_ring[slot][col // (NC // 2)], (rnd + 1) * 16)
                        alone(act)
                    src = ring[slot][col // NC][:, col % NC * CW:(col % NC + 1) * CW]
                    act.drain()
                    nc.scalar.activation(junk, src, ACT.Sign, accum_out=csum[:, col:col + 1])
                    act.drain()
                    last = nc.scalar.activation(junk, src, ACT.Sign, bias=neg_small[:, 0:1], accum_out=cshift[:, col:col + 1])
                last.then_inc(s_cnt, 1)

            neg_small = neg_half[:, 7:8]
            act.wait_ge(s_const, 1)
            check(0, 0, 0)
            act.wait_ge(s_wts, 16 * 14)

            def evac_hT(k):
                act.wait_ge(s_hTp, k + 2)
                nc.scalar.copy(hT, T[0][:, :]).then_inc(s_hT, 1)

            def relu_h1(k):
                act.wait_ge(s_zT, k)
                for f in range(KH):
                    last = nc.scalar.activation(h1T[:, f * BW:(f + 1) * BW], T[f][:, :], ACT.Relu,
                                                bias=gb1[:, KH + f:KH + f + 1], scale=gb1[:, f:f + 1])
                last.then_inc(s_h1T, 1)

            def step(k, slot, rnd, prev, nxt):
                n_slot, n_rnd = 1 - slot, (rnd + 1 if slot == 1 else rnd)
                if nxt:
                    check(k + 1, n_slot, n_rnd)
                if prev:
                    relu_h1(k)
                evac_hT(k)

            peeled(act, step, relu_h1)

            def step2(k, slot, rnd, prev, nxt):
                if not prev:
                    return
                act.wait_ge(s_agg2, k)
                act.wait_ge(s_t2, k)
                nc.scalar.copy(p2T, PA[slot][:, :]).then_inc(s_p2, 1)
                act.wait_ge(s_hn2p, k)
                nc.scalar.copy(hnT, T[1][:, :]).then_inc(s_hn2T, 1)
                act.wait_ge(s_l2, k)
                nc.scalar.activation(ex, lg, ACT.Exp).then_inc(s_ex, 1)

            peeled(act, step2, lambda k: step2(k, 0, 0, True, False))

            def expert(e, par):
                act.wait_ge(s_xTp, e + 1)
                nc.scalar.copy(e_xT[:, 0:BW], T[0][:, :])
                nc.scalar.copy(e_xT[:, BW:CAP], T[1][:, 0:CAP - BW]).then_inc(s_xT, 1)
                for q in range(2 * FK):
                    f, c = q // 2, q % 2
                    act.wait_ge(s_h1, e * (2 * FK) + q + 1)
                    nc.scalar.activation(e_hm[:, f * CAP + c * CAP // 2:f * CAP + (c + 1) * CAP // 2], HB[q % 4][:, 0:CAP // 2],
                                         ACT.Relu, bias=e_b1[par][:, f:f + 1]).then_inc(s_hm, 1)

            act.wait_ge(s_ein[0], 16 * 5)
            with act.Fori(0, E1 // 2) as i:
                for par in range(2):
                    act.wait_ge(s_ein[par], (i + 1) * 80)
                    expert(i * 2 + par, par)

            act.wait_ge(s_wts3, 16 * len(F2_INPUTS))
            act.wait_ge(s_fin2, 1)

            def step3(k, slot, rnd, prev, nxt):
                if not prev:
                    return
                act.wait_ge(s_agg3, k)
                act.wait_ge(s_oTt, k)
                nc.scalar.activation(oT, PA[1 - slot][:, :], ACT.Copy, scale=w_g[:, 0:1]).then_inc(s_oT, 1)
                act.wait_ge(s_hn3p, k)
                nc.scalar.copy(hT3, T[1][:, :]).then_inc(s_hT3, 1)
                act.wait_ge(s_h0p, k)
                for m in range(KH):
                    last = nc.scalar.activation(h_a[:, m * BW:(m + 1) * BW], O[m][:, :], ACT.Relu, bias=b_i[:, m:m + 1])
                last.then_inc(s_h0, 1)
                for n in range(L2 * SB):
                    l, s = n // SB, n % SB
                    dst = (h_b, h_a)[l]
                    if s % SH == 0:
                        act.wait_ge(s_wu, (k - 1) * (L2 * SB) + n + SH + WS)
                        alone(act)
                    e = act.value_load(route_sb[0:1, ds((k - 1) * SB + s, 1)], min_val=0, max_val=E2 - 1)
                    for m in range(KH):
                        at = m * SH * SEG + s % SH * SEG
                        last = nc.scalar.activation(dst[:, m * BW + s * SEG:m * BW + (s + 1) * SEG], LB[n // SH][:, at:at + SEG],
                                                    ACT.Relu, bias=b_r[:, ds(e + (l * KH + m) * E2, 1)])
                    if s % SH == SH - 1:
                        last.then_inc(s_l, 1)

            peeled(act, step3, lambda k: step3(k, 0, 0, True, False))

        @block.gpsimd
        def _(pool):
            nc.gpsimd.memset(ident[:, :], 0.0)
            nc.gpsimd.memset(onesb[:, :], 1.0)
            nc.gpsimd.memset(ones[:, :], 1.0)
            nc.gpsimd.memset(neg_half[:, 0:7], -0.5)
            pool.drain()
            nc.gpsimd.memset(neg_half[:, 7:8], -SMALL)
            nc.gpsimd.affine_select(out=ident[:, :], in_=ident[:, :], compare_op=ALU.not_equal, fill=1.0, base=0,
                                    pattern=[[-1, P]], channel_multiplier=1)
            nc.gpsimd.affine_select(out=tri[:, :], in_=onesb[:, :], compare_op=ALU.is_ge, fill=0.0, base=0,
                                    pattern=[[1, P]], channel_multiplier=-1).then_inc(s_const, 1)

            def inv_sqrt(n, var, s_in, at_in, s_out):
                pool.wait_ge(s_in, at_in)
                alone(pool)
                nc.gpsimd.tensor_scalar(ve[:, 0:n], var, LN_EPS, 0.0, ALU.add, ALU.add)
                pool.drain()
                nc.gpsimd.tensor_tensor(rstd[:, 0:n], ve[:, 0:n], neg_half[:, 0:1].to_broadcast([P, n]), ALU.pow).then_inc(s_out, 1)

            mv8 = tiles(mv[:, :], 8, 2)
            for c in range(4):
                inv_sqrt(8, mv8[:, :, 1], s_mv0, c + 1, s_rstd0)

            def stage(k):
                pool.wait_ge(s_hTp, k + 1)
                alone(pool)
                nc.gpsimd.tensor_copy(hs, S[:, ds(scan(pool, k) * BW, BW)]).then_inc(s_hs, 1)

            def bias_rows(kk):
                pool.wait_ge(s_msp, kk + 1)
                alone(pool)
                for t in range(BT):
                    pool.wait_ge(s_o1u, kk * BT + t + 1)
                    alone(pool)
                    nc.gpsimd.tensor_scalar(pre[t % 2], b_io[:, :], cc[:, t:t + 1], None, ALU.mult)
                    pool.drain()
                    nc.gpsimd.tensor_tensor(pre[t % 2], pre[t % 2], b_all[:, :], ALU.add).then_inc(s_pre, 1)

            def tail(k):
                bias_rows(k - 1)
                inv_sqrt(BT, mv8[:, 0:BT, 1], s_mv, k, s_rstd)

            def step(k, slot, rnd, prev, nxt):
                stage(k)
                if prev:
                    tail(k)
                pool.wait_ge(s_msp, k + 1)
                alone(pool)
                pool.wait_ge(s_hT, k + 1)
                alone(pool)
                nc.gpsimd.tensor_tensor(aT, aT, hT, ALU.mult).then_inc(s_neh, 1)

            pool.wait_ge(s_hn, 4)
            pool.wait_ge(s_wready, 1)
            peeled(pool, step, tail)

            pool.wait_ge(s_u2u, 2 + 2 * NB)
            nc.gpsimd.iota(w8, pattern=[[0, BT], [-1, E1]], base=E1, channel_multiplier=0, allow_small_or_imprecise_dtypes=True)
            nc.gpsimd.iota(cofs, pattern=[[0, BT], [CAP, E1]], base=-1, channel_multiplier=0, allow_small_or_imprecise_dtypes=True)
            nc.gpsimd.iota(tok, pattern=[[P, BT]], base=0, channel_multiplier=1, allow_small_or_imprecise_dtypes=True)
            nc.gpsimd.memset(off[:, 0:E1], 0.0).then_inc(s_const, 1)
            pool.wait_ge(s_fill, 80)

            def step2(k, slot, rnd, prev, nxt):
                if not prev:
                    return
                inv_sqrt(BT, mv8[:, 0:BT, 1], s_mv2, k * 2 - 1, s_rstd2)
                inv_sqrt(BT, mv8[:, 0:BT, 1], s_mv2, k * 2, s_rstd2)
                pool.wait_ge(s_idx, k)
                alone(pool)
                for t in range(BT):
                    nc.gpsimd.indirect_dma_start(disp_d, bass.IndirectOffsetOnAxis(ap=idx[:, t:t + 1], axis=0),
                                                 rows[:, t * ROW:(t + 1) * ROW], None,
                                                 bounds_check=E1 * CAP - 1, oob_is_err=False).then_inc(s_sc, 16)

            peeled(pool, step2, lambda k: step2(k, 0, 0, True, False))

            with pool.Fori(0, E1 // 2) as i:
                for par in range(2):
                    pool.wait_ge(s_y, i * 2 + par + 3)
                    alone(pool)
                    for q in range(CT):
                        nc.gpsimd.indirect_dma_start(y_d, bass.IndirectOffsetOnAxis(ap=e_idx[par][:, q:q + 1], axis=0),
                                                     e_y[par][:, q * D:(q + 1) * D], None,
                                                     bounds_check=N - 1, oob_is_err=False).then_inc(s_sc2[par], 16)
            for c in range(4):
                inv_sqrt(8, mv8[:, :, 1], s_mv3, c + 1, s_rstd3)

            def step3(k, slot, rnd, prev, nxt):
                if not prev:
                    return
                inv_sqrt(BT, mv8[:, 0:BT, 1], s_mv4, k, s_rstd4)
                pool.wait_ge(s_hn3, k)
                alone(pool)
                nc.gpsimd.tensor_tensor(tiles(x3), tiles(x3), b_o.unsqueeze(1).to_broadcast([P, BT, D]), ALU.add).then_inc(s_x3b, 1)
                pool.wait_ge(s_out, k)
                alone(pool)
                nc.gpsimd.dma_start(out_t[:, ds((k - 1) * BT, BT), :], tiles(ob)).then_inc(s_stored, 16)

            peeled(pool, step3, lambda k: step3(k, 0, 0, True, False))

        @block.vector
        def _(dve):
            mv8 = tiles(mv[:, :], 8, 2)

            def stats(tile_of, n):
                for t in range(n):
                    nc.vector.bn_stats(st6[:, 6 * t:6 * t + 6], tile_of(t))
                dve.drain()
                for t in range(n):
                    last = nc.vector.bn_aggr(mv8[:, t, :], st6[:, 6 * t:6 * t + 6])
                return last

            nc.vector.memset(U[:, :], 0.0)
            nc.vector.memset(fill, 0.0)
            dve.drain()
            nc.vector.memset(tiles(fill, 10, ROW)[:, :, D + 1], NOWHERE).then_inc(s_zero, 1)
            nc.vector.memset(small[:, 28:32], 0.0).then_inc(s_aT, 2)
            nc.vector.memset(sumc, 0.0).then_inc(s_o1u, 2)
            nc.vector.memset(rbp, 0.0).then_inc(s_u2u, 2)
            nc.vector.memset(cc, 0.0).then_inc(s_hTp, 1)
            nc.vector.memset(rs_, 0.0).then_inc(s_bad, 1)
            nc.vector.memset(ws_, 0.0).then_inc(s_p2, 2)
            nc.vector.memset(nn, 0.0).then_inc(s_t2, 1)
            nc.vector.memset(rw_, 0.0).then_inc(s_x1, 1)
            for c in range(4):
                dve.wait_ge(s_xin[c], 16)
                stats(lambda t: S[:, (8 * c + t) * D:(8 * c + t + 1) * D], 8).then_inc(s_mv0, 1)
                dve.wait_ge(s_rstd0, c + 1)
                alone(dve)
                for t in range(8):
                    tile = S[:, (8 * c + t) * D:(8 * c + t + 1) * D]
                    last = nc.vector.tensor_scalar(tile, tile, mv8[:, t, 0:1], rstd[:, t:t + 1], ALU.subtract, ALU.mult)
                last.then_inc(s_hn, 1)
                dve.drain()
            dve.wait_ge(s_wts, 16 * 14)
            nc.vector.tensor_tensor(b_all[:, :], b_all[:, :], t_bs1, ALU.add)
            nc.vector.tensor_tensor(b_us[:, D:2 * D], b_us[:, D:2 * D], t_bs2, ALU.add)
            dve.wait_ge(s_wprod, 1)
            nc.vector.tensor_copy(W_io[:, :], O[0][:, 0:DH])
            nc.vector.tensor_copy(b_io[:, :], O[0][:, DH:2 * DH])
            nc.vector.tensor_copy(W_us[:, :, 0:D], tiles(O[1][:, 0:2 * D], KH))
            nc.vector.tensor_copy(b_us[:, 0:D], O[1][:, 2 * D:3 * D]).then_inc(s_wready, 1)

            def reduce_half(dst, slot, h):
                nc.vector.tensor_reduce(dst, ring[slot][h].rearrange("p (t c) -> p c t", t=HT, c=BW), AX.X, ALU.add)

            def sum_halves():
                dve.drain()
                nc.vector.tensor_tensor(pA, pA, thr, ALU.add).then_inc(s_part, 1)

            def partials(k, slot, rnd, h):
                if not isinstance(k, int) or k > 0:
                    if h == 0:
                        dve.wait_ge(s_ms, k)
                    else:
                        dve.wait_ge(s_thrst, k * 16)
                    alone(dve)
                for q in range(2 * h, 2 * h + 2):
                    dve.wait_ge(s_ring[slot][q], (rnd + 1) * 16)
                    alone(dve)
                reduce_half((pA, thr)[h], slot, h)

            def mask_block(slot, th, tmp):
                for h in range(2):
                    with dve.Fori(0, HT) as t:
                        piece = ring[slot][h][:, ds(t * BW, BW)]
                        nc.vector.tensor_tensor(tmp, piece, th, ALU.is_gt)
                        dve.drain()
                        nc.vector.tensor_tensor(piece, piece, tmp, ALU.mult)
                        dve.drain()

            def verdict(k):
                dve.wait_ge(s_sums, k + 1)
                alone(dve)
                nc.vector.tensor_scalar(thr, SR[:, :], EPS, THRESH, ALU.add, ALU.mult)
                nc.vector.tensor_scalar(sumc, SM[:, 0:BT], EPS, None, ALU.add)
                dve.drain()
                nc.vector.tensor_reduce(smax, thr, AX.X, ALU.max).then_inc(s_thr, 1)
                dve.wait_ge(s_cnt, k + 1)
                alone(dve)
                nc.vector.scalar_tensor_tensor(junk_c, csum, -2.0, cshift, ALU.mult, ALU.add, accum_out=cdiff)
                dve.drain()
                nc.vector.tensor_scalar(bad1, cdiff, float(-2 * HALF), None, ALU.not_equal)
                dve.drain()
                nc.vector.scalar_tensor_tensor(bad, smax, SMALL, bad1, ALU.is_ge, ALU.add).then_inc(s_bad, 1)

            junk_c = ve[:, 0:2 * NC]
            junk_c = small[:, 64:64 + 2 * NC]

            def mask_if_needed(k, slot):
                blk = scan(dve, k)
                dve.wait_ge(s_flag, k + 1)
                alone(dve)
                nc.vector.tensor_copy(flags[0:1, ds(blk, 1)], SM[0:1, 2 * BT:2 * BT + 1])
                dve.drain()
                flag = dve.value_load(flags[0:1, ds(blk, 1)], min_val=0, max_val=2 * P)
                with dve.If(flag > 0):
                    mask_block(slot, thr, pA)
                    reduce_half(pA, slot, 0)
                    dve.wait_ge(s_thrst, k * 16 + 16)
                    alone(dve)
                    reduce_half(thr, slot, 1)
                    dve.drain()
                    nc.vector.tensor_tensor(pA, pA, thr, ALU.add)
                    dve.drain()
                dve.drain().then_inc(s_clean, 1)

            def scales(k):
                blk = scan(dve, k)
                dve.wait_ge(s_ms, k + 1)
                alone(dve)
                ms = SM[:, BT:2 * BT]
                nc.vector.tensor_scalar(aT, SR[:, :], 0.0, None, ALU.is_le)
                nc.vector.reciprocal(rs_, sumc)
                nc.vector.tensor_scalar(nn, ms, 0.0, None, ALU.is_gt)
                nc.vector.tensor_scalar(ne[:, ds(blk * BT, BT)], ms, 0.0, None, ALU.is_le)
                nc.vector.tensor_scalar(cc, ms, 0.0, None, ALU.is_le)
                dve.drain()
                nc.vector.tensor_tensor(ws_, ms, rs_, ALU.mult)
                dve.drain()
                nc.vector.tensor_scalar(rw_, ws_, EPS, None, ALU.add)
                dve.drain()
                nc.vector.reciprocal(rw_, rw_)
                dve.drain()
                nc.vector.tensor_tensor(rs_, rs_, rw_, ALU.mult)
                nc.vector.tensor_tensor(ws_, ws_, rw_, ALU.mult)
                dve.drain()
                nc.vector.tensor_copy(rb[:, ds(blk * BT, BT)], rs_)
                nc.vector.tensor_tensor(rbp, rs_, nn, ALU.mult)
                dve.drain()
                nc.vector.tensor_tensor(rbp, rbp, cc, ALU.add)
                dve.drain()
                nc.vector.tensor_tensor(cc, cc, ws_, ALU.add).then_inc(s_msp, 1)

            def normalise(k):
                for t in range(BT):
                    zt = z1[:, t * DH:(t + 1) * DH]
                    bank = O[t % 2]
                    n = (k - 1) * BT + t + 1
                    dve.wait_ge(s_o1, n)
                    alone(dve)
                    dve.wait_ge(s_pre, n)
                    alone(dve)
                    nc.vector.tensor_tensor(zt, bank[:, DH:2 * DH], pre[t % 2], ALU.add)
                    dve.drain()
                    nc.vector.scalar_tensor_tensor(zt, bank[:, 0:DH], rbp[:, t:t + 1], zt, ALU.mult, ALU.add).then_inc(s_o1u, 1)
                    dve.drain()
                stats(lambda t: z1[:, t * DH:(t + 1) * DH], BT).then_inc(s_mv, 1)
                dve.wait_ge(s_rstd, k)
                alone(dve)
                for t in range(BT):
                    zt = z1[:, t * DH:(t + 1) * DH]
                    last = nc.vector.tensor_scalar(zt, zt, mv8[:, t, 0:1], rstd[:, t:t + 1], ALU.subtract, ALU.mult)
                last.then_inc(s_z, 1)

            def layer2_inputs(k):
                blk = scan(dve, k - 1)
                dve.drain()
                for u in range(2):
                    dve.wait_ge(s_u2, (k - 1) * 2 + u + 1)
                    alone(dve)
                    src = O[u].rearrange("p (t c) -> p t c", t=2, c=2 * D)
                    cols = ds(blk * BW + u * 2 * D, 2 * D)
                    nc.vector.tensor_tensor(tiles(U[:, cols], 2), src[:, :, 0:D], b_us[:, 0:D].unsqueeze(1).to_broadcast([P, 2, D]), ALU.add)
                    nc.vector.tensor_tensor(tiles(R[:, cols], 2), src[:, :, D:2 * D], b_us[:, D:2 * D].unsqueeze(1).to_broadcast([P, 2, D]),
                                            ALU.add).then_inc(s_u2u, 1)
                dve.drain()
                for t in range(BT):
                    cols = ds(blk * BW + t * D, D)
                    nc.vector.scalar_tensor_tensor(R[:, cols], U[:, cols], ne[:, ds(blk * BT + t, 1)], R[:, cols], ALU.mult, ALU.add)

            def collect(k):
                dve.wait_ge(s_agg, k)
                alone(dve)
                dve.wait_ge(s_neh, k)
                alone(dve)

            def step(k, slot, rnd, prev, nxt):
                n_slot, n_rnd = 1 - slot, (rnd + 1 if slot == 1 else rnd)
                if prev:
                    collect(k)
                    nc.vector.tensor_tensor(aT, PA[1 - slot][:, :], aT, ALU.add).then_inc(s_aT, 1)
                if nxt:
                    partials(k + 1, n_slot, n_rnd, 0)
                if prev:
                    normalise(k)
                scales(k)
                if nxt:
                    partials(k + 1, n_slot, n_rnd, 1)
                    sum_halves()
                    verdict(k + 1)
                    mask_if_needed(k + 1, n_slot)
                if prev:
                    layer2_inputs(k)

            for h in range(2):
                partials(0, 0, 0, h)
            sum_halves()
            verdict(0)
            mask_if_needed(0, 0)
            dve.wait_ge(s_fill, 80)

            step(0, 0, 0, False, True)
            with dve.Fori(0, NB // 2 - 1) as i:
                step(i * 2 + 1, 1, i, True, True)
                step(i * 2 + 2, 0, i + 1, True, True)
            step(NB - 1, 1, NB // 2 - 1, True, False)
            collect(NB)
            nc.vector.tensor_tensor(aT, PA[1][:, :], aT, ALU.add).then_inc(s_aT, 1)
            normalise(NB)
            layer2_inputs(NB)
            dve.drain()

            def mask2(j, slot, landed):
                if landed is not None:
                    for q in range(4):
                        dve.wait_ge(s_ring[slot][q], landed)
                        alone(dve)
                flag = dve.value_load(flags[0:1, ds(j, 1)], min_val=0, max_val=2 * P)
                with dve.If(flag > 0):
                    mask_block(slot, thr2[slot], msk)
                dve.drain().then_inc(s_clean2, 1)

            def lnorm(k, which, src, dst_of):
                stats(src, BT).then_inc(s_mv2, 1)
                dve.wait_ge(s_rstd2, k * 2 - 1 + which)
                alone(dve)
                for t in range(BT):
                    last = nc.vector.tensor_scalar(dst_of(t), src(t), mv8[:, t, 0:1], rstd[:, t:t + 1],
                                                   ALU.subtract, ALU.mult)
                return last

            def bc3(ap):
                return ap.unsqueeze(1).to_broadcast([P, BT, D])

            def e3(ap):
                return tiles(ap, BT, E1)

            def bce(ap):
                return ap.unsqueeze(2).to_broadcast([P, BT, E1])

            rows3 = tiles(rows, BT, ROW)

            def route(k):
                j = k - 1
                nc.vector.tensor_copy(rb4, rb[:, ds(j * BT, BT)])
                dve.wait_ge(s_t2, k + 1)
                alone(dve)
                dve.drain()
                for t in range(BT):
                    c = slice(t * D, (t + 1) * D)
                    last = nc.vector.scalar_tensor_tensor(o2[:, c], T[0][:, c], rb4[:, t:t + 1], R[:, ds(j * BW + t * D, D)], ALU.mult, ALU.add)
                last.then_inc(s_t2u, 1)
                dve.drain()
                lnorm(k, 0, lambda t: o2[:, t * D:(t + 1) * D], lambda t: o2[:, t * D:(t + 1) * D])
                dve.drain()
                nc.vector.tensor_tensor(tiles(o2), tiles(o2), bc3(g2), ALU.mult)
                dve.drain()
                nc.vector.tensor_tensor(tiles(o2), tiles(o2), bc3(be2), ALU.add)
                dve.drain()
                dve.wait_ge(s_xb, k * 16)
                alone(dve)
                x1 = S[:, ds(j * BW, BW)]
                nc.vector.scalar_tensor_tensor(x1, o2, 0.0, xb, ALU.max, ALU.add).then_inc(s_x1, 1)
                dve.drain()
                if not isinstance(k, int) or k > 1:
                    dve.wait_ge(s_sc, k * 64 - 64)
                    alone(dve)
                lnorm(k, 1, lambda t: S[:, ds(j * BW + t * D, D)], lambda t: rows[:, t * ROW:t * ROW + D]).then_inc(s_hn2, 1)
                dve.wait_ge(s_lg, k)
                alone(dve)
                nc.vector.tensor_tensor(lg, SR[:, 0:BT * E1], gbc, ALU.add)
                dve.drain()
                nc.vector.tensor_reduce(lmax, e3(lg), AX.X, ALU.max)
                dve.drain()
                nc.vector.tensor_tensor(e3(lg), e3(lg), bce(lmax), ALU.subtract).then_inc(s_l2, 1)
                dve.wait_ge(s_ex, k)
                alone(dve)
                nc.vector.tensor_reduce(esum, e3(ex), AX.X, ALU.add)
                nc.vector.tensor_reduce(lmax, e3(ex), AX.X, ALU.max)
                dve.drain()
                nc.vector.reciprocal(esum, esum)
                nc.vector.tensor_tensor(e3(sc), e3(ex), bce(lmax), ALU.is_equal)
                dve.drain()
                nc.vector.tensor_tensor(rows3[:, :, D], lmax, esum, ALU.mult)
                nc.vector.tensor_tensor(sc, sc, w8, ALU.mult)
                nc.vector.tensor_copy(rows3[:, :, D + 1], tok)
                dve.drain()
                nc.vector.tensor_reduce(lmax, e3(sc), AX.X, ALU.max)
                nc.vector.tensor_scalar(tok, tok, float(BW), None, ALU.add)
                dve.drain()
                nc.vector.tensor_tensor(e3(oh), e3(sc), bce(lmax), ALU.is_equal).then_inc(s_oh, 1)
                dve.wait_ge(s_cum, k)
                alone(dve)
                for t in range(BT):
                    nc.vector.tensor_tensor(off[:, (t + 1) * E1:(t + 2) * E1], SM[:, (BT + t) * E1:(BT + t + 1) * E1],
                                            off[:, t * E1:(t + 1) * E1], ALU.add)
                    dve.drain()
                nc.vector.tensor_tensor(cw, SM[:, 0:BT * E1], off[:, 0:BT * E1], ALU.add)
                dve.drain()
                nc.vector.tensor_copy(off[:, 0:E1], off[:, BT * E1:(BT + 1) * E1])
                nc.vector.tensor_scalar(sc, cw, float(CAP), NOWHERE, ALU.is_gt, ALU.mult)
                nc.vector.tensor_tensor(cw, cw, cofs, ALU.add)
                dve.drain()
                nc.vector.tensor_tensor(cw, cw, sc, ALU.add)
                dve.drain()
                nc.vector.tensor_tensor(cw, cw, oh, ALU.mult)
                dve.drain()
                nc.vector.tensor_reduce(slot_f, e3(cw), AX.X, ALU.add)
                dve.drain()
                nc.vector.tensor_copy(idx, slot_f).then_inc(s_idx, 1)
                dve.drain()

            slot_f = slot
            dve.wait_ge(s_const, 2)
            dve.wait_ge(s_wts2, 48)
            for j in range(2):
                dve.wait_ge(s_thr2[1 - j], 16)
                mask2(j, 1 - j, None)
            def step2(k, slot, rnd, n_rnd):
                dve.wait_ge(s_thr2[slot], n_rnd * 16 + 16)
                alone(dve)
                mask2(k + 1, slot, n_rnd * 16 + 64)
                route(k)

            with dve.Fori(0, NB // 2 - 1) as i:
                step2(i * 2 + 1, 1, i, i + 1)
                step2(i * 2 + 2, 0, i, i + 1)
            route(NB - 1)
            route(NB)

            dve.wait_ge(s_agg2, NB)
            nc.vector.memset(small[:, 0:4], 0.0).then_inc(s_y, 2)
            nc.vector.memset(small[:, 4:8], 0.0).then_inc(s_hm, 4)
            nc.vector.memset(small[:, 12:16], 0.0).then_inc(s_ye, 1)
            nc.vector.memset(small[:, 16:20], 0.0).then_inc(s_oT, 2)
            nc.vector.memset(small[:, 20:24], 0.0).then_inc(s_oTt, 1)
            nc.vector.memset(small[:, 24:28], 0.0).then_inc(s_wu, WS)

            def expert(e, par, rnd):
                y, er = e_y[par], tiles(e_rows[par], CT, ROW)
                y5 = tiles(y, CT)
                dve.wait_ge(s_yp, e + 1)
                alone(dve)
                if rnd is not None:
                    dve.wait_ge(s_sc2[par], rnd * (16 * CT))
                    alone(dve)
                nc.vector.tensor_tensor(y5[:, 0:BT, :], tiles(O[0][:, :]), e_b2[par].unsqueeze(1).to_broadcast([P, BT, D]), ALU.add)
                nc.vector.tensor_tensor(y5[:, BT, :], O[1][:, 0:D], e_b2[par], ALU.add).then_inc(s_ye, 1)
                nc.vector.tensor_copy(e_idx[par], er[:, :, D + 1])
                dve.drain()
                for q in range(CT):
                    nc.vector.tensor_scalar(y5[:, q, :], y5[:, q, :], er[:, q, D:D + 1], None, ALU.mult)
                dve.drain()
                nc.vector.tensor_scalar(e_fin, y, 0.0, 0.0, ALU.mult, ALU.is_equal)
                nc.vector.tensor_scalar(e_pos, y, FMAX, BIG, ALU.is_gt, ALU.mult)
                nc.vector.tensor_scalar(e_neg, y, -FMAX, -BIG, ALU.is_lt, ALU.mult)
                dve.drain()
                nc.vector.tensor_scalar(y, y, FMAX, -FMAX, ALU.min, ALU.max)
                dve.drain()
                nc.vector.tensor_tensor(y, y, e_fin, ALU.mult)
                dve.drain()
                nc.vector.tensor_tensor(y, y, e_pos, ALU.add)
                dve.drain()
                nc.vector.tensor_tensor(y, y, e_neg, ALU.add).then_inc(s_y, 1)
                dve.drain()

            expert(0, 0, None)
            expert(1, 1, None)
            with dve.Fori(1, E1 // 2) as i:
                expert(i * 2, 0, i)
                expert(i * 2 + 1, 1, i)

            dve.wait_ge(s_wts3, 16 * len(F2_INPUTS))
            for l in range(L2):
                for kk in range(KH):
                    diag = w_s[:, (l * KH + kk) * DH + kk * P:(l * KH + kk) * DH + (kk + 1) * P]
                    nc.vector.tensor_tensor(diag, diag, ident[:, :], ALU.add)
                    lm = l * KH + kk
                    nc.vector.tensor_scalar(b_r[:, lm * E2:(lm + 1) * E2], b_r[:, lm * E2:(lm + 1) * E2], b_s[:, lm:lm + 1], None, ALU.add)
            dve.drain().then_inc(s_fin2, 1)

            for c in range(4):
                cols = slice(c * 1024, (c + 1) * 1024)
                dve.wait_ge(s_yin[c], 16)
                nc.vector.tensor_tensor(R[:, cols], R[:, cols], S[:, cols], ALU.add)
                dve.drain()
                stats(lambda t: R[:, (8 * c + t) * D:(8 * c + t + 1) * D], 8).then_inc(s_mv3, 1)
                dve.wait_ge(s_rstd3, c + 1)
                for t in range(8):
                    tc = slice((8 * c + t) * D, (8 * c + t + 1) * D)
                    last = nc.vector.tensor_scalar(S[:, tc], R[:, tc], mv8[:, t, 0:1], rstd[:, t:t + 1], ALU.subtract, ALU.mult)
                last.then_inc(s_hid, 1)
                dve.drain()

            dve.wait_ge(s_ring[0][0], 16 * 8)
            dve.wait_ge(s_ring[0][2], 16 * 8)

            def stage_w(k, l, s):
                n = l * SB + s
                dve.wait_ge(s_wu, (k - 1) * (L2 * SB) + n + 1)
                alone(dve)
                e = dve.value_load(route_sb[0:1, ds((k - 1) * SB + s, 1)], min_val=0, max_val=E2 - 1)
                nc.vector.tensor_tensor(wst[n % WS], ring[0][l][:, ds(e * (KH * DH), KH * DH)],
                                        w_s[:, l * KH * DH:(l + 1) * KH * DH], ALU.add).then_inc(s_wst, 1)

            def step3(k):
                for s in range(WS):
                    stage_w(k, 0, s)
                dve.wait_ge(s_oTt, k + 1)
                alone(dve)
                nc.vector.tensor_tensor(x3, T[0][:, :], R[:, ds((k - 1) * BW, BW)], ALU.add).then_inc(s_x3, 1)
                dve.drain()
                stats(lambda t: x3[:, t * D:(t + 1) * D], BT).then_inc(s_mv4, 1)
                dve.wait_ge(s_rstd4, k)
                alone(dve)
                for t in range(BT):
                    c = slice(t * D, (t + 1) * D)
                    last = nc.vector.tensor_scalar(hn3[:, c], x3[:, c], mv8[:, t, 0:1], rstd[:, t:t + 1], ALU.subtract, ALU.mult)
                last.then_inc(s_hn3, 1)
                for n in range(WS, L2 * SB):
                    stage_w(k, n // SB, n % SB)
                dve.wait_ge(s_fin, k)
                alone(dve)
                dve.wait_ge(s_x3b, k)
                alone(dve)
                if not isinstance(k, int) or k > 1:
                    dve.wait_ge(s_stored, k * 16 - 16)
                    alone(dve)
                nc.vector.tensor_tensor(ob, T[0][:, :], x3, ALU.add).then_inc(s_out, 1)
                dve.drain()

            with dve.Fori(0, NB // 2) as i:
                step3(i * 2 + 1)
                step3(i * 2 + 2)

        @block.tensor
        def _(pe):
            pe.wait_ge(s_wts, 16 * 14)
            pe.wait_ge(s_const, 1)
            for kk in range(KH):
                nc.tensor.matmul(O[0][:, 0:DH], t_in1T[:, kk * P:(kk + 1) * P], t_out1[:, kk * DH:(kk + 1) * DH], start=kk == 0, stop=kk == KH - 1)
            for kk in range(KH):
                nc.tensor.matmul(O[0][:, DH:2 * DH], t_bin1[:, kk * P:(kk + 1) * P], t_out1[:, kk * DH:(kk + 1) * DH], start=kk == 0, stop=kk == KH - 1)
            for kk in range(KH):
                nc.tensor.matmul(O[1][:, kk * D:(kk + 1) * D], t_in2T[:, kk * P:(kk + 1) * P], t_out2, start=True, stop=True)
            nc.tensor.matmul(O[1][:, 2 * D:3 * D], t_bin2, t_out2, start=True, stop=True).then_inc(s_wprod, 1)

            def sums(cols, s):
                nc.tensor.matmul(SR[:, :], ones[:, :], pA, start=True, stop=True)
                for t in range(BT):
                    last = nc.tensor.matmul(SM[:, cols + t:cols + t + 1], pA[:, t * P:(t + 1) * P], ones[:, 0:1], start=True, stop=True)
                last.then_inc(s, 1)

            def raw_sums(k, first=False):
                pe.wait_ge(s_part, k + 1)
                if not first:
                    pe.wait_ge(s_msp, k)
                sums(0, s_sums)

            def sum_verdict(k):
                pe.wait_ge(s_bad, k + 2)
                nc.tensor.matmul(SM[0:1, 2 * BT:2 * BT + 1], bad, ones[:, 0:1], start=True, stop=True).then_inc(s_flag, 1)

            def products(X, slot, lo, hi, s_quarter):
                for t in range(lo, hi):
                    mm = nc.tensor.matmul(PA[slot][:, :], X[:, t * D:(t + 1) * D], ring[slot][t // HT][:, (t % HT) * BW:(t % HT + 1) * BW],
                                          start=t == 0, stop=t == NT - 1)
                    if t % QT == QT - 1 and t < NT - 1:
                        mm.then_inc(s_quarter, 1)
                return mm

            def out_rows(k):
                pe.wait_ge(s_aT, k + 2)
                for t in range(BT):
                    if t < 2:
                        pe.wait_ge(s_u2u, (k - 1) * 2 + t + 1)
                    else:
                        pe.wait_ge(s_o1u, (k - 1) * BT + t + 1)
                    nc.tensor.matmul(O[t % 2][:, 0:DH], aT[:, t * P:(t + 1) * P], W_io[:, :], start=True, stop=True)
                    nc.tensor.matmul(O[t % 2][:, DH:2 * DH], hT[:, t * P:(t + 1) * P], W_s1[:, :], start=True, stop=True).then_inc(s_o1, 1)

            def turn_h(k):
                pe.wait_ge(s_hs, k + 1)
                for t in range(BT):
                    last = nc.tensor.transpose(T[0][:, t * P:(t + 1) * P], hs[:, t * P:(t + 1) * P], ident[:, :])
                last.then_inc(s_hTp, 1)

            def turn_z(k):
                pe.wait_ge(s_z, k)
                for f in range(KH):
                    for t in range(BT):
                        last = nc.tensor.transpose(T[f][:, t * P:(t + 1) * P], z1[:, t * DH + f * P:t * DH + (f + 1) * P], ident[:, :])
                last.then_inc(s_zT, 1)

            def layer2_products(k):
                pe.wait_ge(s_h1T, k)
                for t in range(BT):
                    if t % 2 == 0:
                        pe.wait_ge(s_o1u, (k - 1) * BT + t // 2 + 5)
                    o = O[t // 2][:, (t % 2) * 2 * D:(t % 2 + 1) * 2 * D]
                    for f in range(KH):
                        mm = nc.tensor.matmul(o, h1T[:, f * BW + t * P:f * BW + (t + 1) * P], W_us[:, f, :], start=f == 0, stop=f == KH - 1)
                    if t % 2 == 1:
                        mm.then_inc(s_u2, 1)

            def step(k, slot, rnd, prev, nxt):
                pe.wait_ge(s_clean, k + 1)
                sums(BT, s_ms)
                pe.wait_ge(s_aT, k + 1)
                products(S, slot, 0, QT, s_quart)
                if prev:
                    out_rows(k)
                products(S, slot, QT, 3 * QT, s_quart)
                if prev:
                    pe.wait_ge(s_hT, k)
                    turn_z(k)
                products(S, slot, 3 * QT, 3 * QT + QT // 2, s_quart)
                if nxt:
                    raw_sums(k + 1)
                products(S, slot, 3 * QT + QT // 2, NT, s_quart).then_inc(s_agg, 1)
                if nxt:
                    sum_verdict(k + 1)
                if prev:
                    layer2_products(k)
                turn_h(k)

            def last_tail(k):
                out_rows(k)
                turn_z(k)
                layer2_products(k)

            raw_sums(0, True)
            sum_verdict(0)
            pe.wait_ge(s_hn, 4)
            pe.wait_ge(s_wready, 1)
            peeled(pe, step, last_tail)

            def tail_a(k):
                pe.wait_ge(s_p2, k + 2)
                if not isinstance(k, int) or k > 1:
                    pe.wait_ge(s_t2u, k - 1)
                for t in range(BT):
                    last = nc.tensor.transpose(T[0][:, t * P:(t + 1) * P], p2T[:, t * P:(t + 1) * P], ident[:, :])
                last.then_inc(s_t2, 1)

            def tail_b(k):
                pe.wait_ge(s_hn2, k)
                for t in range(BT):
                    last = nc.tensor.transpose(T[1][:, t * P:(t + 1) * P], rows[:, t * ROW:t * ROW + D], ident[:, :])
                last.then_inc(s_hn2p, 1)

            def tail_c(k):
                pe.wait_ge(s_hn2T, k)
                for t in range(BT):
                    last = nc.tensor.matmul(SR[:, t * E1:(t + 1) * E1], hnT[:, t * P:(t + 1) * P], wgate[:, :], start=True, stop=True)
                last.then_inc(s_lg, 1)

            def tail_d(k):
                pe.wait_ge(s_oh, k)
                nc.tensor.matmul(SM[:, 0:BT * E1], tri[:, :], oh, start=True, stop=True)
                nc.tensor.matmul(SM[:, BT * E1:2 * BT * E1], onesb[:, :], oh, start=True, stop=True).then_inc(s_cum, 1)

            def step2(k, slot, rnd, prev, nxt):
                sl = 1 - slot
                pe.wait_ge(s_clean2, k + 1)
                pe.wait_ge(s_p2, k + 1)
                products(U, sl, 0, QT, s_quart2)
                if prev:
                    tail_a(k)
                products(U, sl, QT, 2 * QT, s_quart2)
                products(U, sl, 2 * QT, 3 * QT, s_quart2)
                if prev:
                    tail_b(k)
                products(U, sl, 3 * QT, 3 * QT + QT // 2, s_quart2)
                if prev:
                    tail_c(k)
                products(U, sl, 3 * QT + QT // 2, NT, s_quart2).then_inc(s_agg2, 1)
                if prev:
                    tail_d(k)

            def last2(k):
                tail_a(k)
                tail_b(k)
                tail_c(k)
                tail_d(k)

            peeled(pe, step2, last2)

            def expert(e, par):
                xr = e_rows[par]
                for q in range(CT):
                    bank, c = (T[0], q) if q < BT else (T[1], 0)
                    last = nc.tensor.transpose(bank[:, c * P:(c + 1) * P], xr[:, q * ROW:q * ROW + D], ident[:, :])
                last.then_inc(s_xTp, 1)
                pe.wait_ge(s_xT, e + 1)
                for q in range(2 * FK):
                    f, c = q // 2, q % 2
                    pe.wait_ge(s_hm, e * (2 * FK) + q + 1)
                    nc.tensor.matmul(HB[q % 4][:, 0:CAP // 2], e_w1[par][:, f * P:(f + 1) * P], e_xT[:, c * CAP // 2:(c + 1) * CAP // 2],
                                     start=True, stop=True).then_inc(s_h1, 1)
                pe.wait_ge(s_hm, e * (2 * FK) + 2 * FK + 4)
                pe.wait_ge(s_ye, e + 1)
                for q in range(CT):
                    bank, c = (O[0], q) if q < BT else (O[1], 0)
                    for f in range(FK):
                        mm = nc.tensor.matmul(bank[:, c * D:(c + 1) * D], e_hm[:, f * CAP + q * P:f * CAP + (q + 1) * P],
                                              e_w2[par][:, f * D:(f + 1) * D], start=f == 0, stop=f == FK - 1)
                mm.then_inc(s_yp, 1)

            pe.wait_ge(s_ex, NB)
            with pe.Fori(0, E1 // 2) as i:
                for par in range(2):
                    pe.wait_ge(s_ein[par], (i + 1) * 80)
                    expert(i * 2 + par, par)

            def products3(k, slot, lo, hi):
                for t in range(lo, hi):
                    if t % QT == 0 and isinstance(k, int) and k == 0:
                        pe.wait_ge(s_hid, t // QT + 1)
                    if t % QT == 0:
                        pe.wait_ge(s_ring[1][t // QT], k * 16 + 128)
                    mm = nc.tensor.matmul(PA[slot][:, :], S[:, t * D:(t + 1) * D], ring[1][t // HT][:, (t % HT) * BW:(t % HT + 1) * BW],
                                          start=t == 0, stop=t == NT - 1)
                    if t % QT == QT - 1 and t < NT - 1:
                        mm.then_inc(s_quart3, 1)
                return mm

            def turn_sum(k):
                pe.wait_ge(s_oT, k + 2)
                if not isinstance(k, int) or k > 1:
                    pe.wait_ge(s_out, k - 1)
                for t in range(BT):
                    last = nc.tensor.transpose(T[0][:, t * P:(t + 1) * P], oT[:, t * P:(t + 1) * P], ident[:, :])
                last.then_inc(s_oTt, 1)

            def turn_hn3(k):
                pe.wait_ge(s_hn3, k)
                for t in range(BT):
                    last = nc.tensor.transpose(T[1][:, t * P:(t + 1) * P], hn3[:, t * P:(t + 1) * P], ident[:, :])
                last.then_inc(s_hn3p, 1)

            def h0(k):
                pe.wait_ge(s_hT3, k)
                for m in range(KH):
                    last = nc.tensor.matmul(O[m][:, :], w_i[:, m * P:(m + 1) * P], hT3, start=True, stop=True)
                last.then_inc(s_h0p, 1)

            def routed(k, g):
                l, half = g * SH // SB, g % (SB // SH)
                src = (h_a, h_b)[l]
                if g == 0:
                    pe.wait_ge(s_h0, k)
                if l == 1:
                    pe.wait_ge(s_l, (k - 1) * NG + g - SB // SH + 1)
                for s in range(half * SH, (half + 1) * SH):
                    n = l * SB + s
                    pe.wait_ge(s_wst, (k - 1) * (L2 * SB) + n + 1)
                    for m in range(KH):
                        at = m * SH * SEG + s % SH * SEG
                        for kk in range(KH):
                            mm = nc.tensor.matmul(LB[g][:, at:at + SEG], wst[n % WS][:, kk * DH + m * P:kk * DH + (m + 1) * P],
                                                  src[:, kk * BW + s * SEG:kk * BW + (s + 1) * SEG], start=kk == 0, stop=kk == KH - 1)
                    mm.then_inc(s_wu, 1)

            def out_proj(k):
                pe.wait_ge(s_l, k * NG)
                for t in range(BT):
                    for kk in range(KH):
                        mm = nc.tensor.matmul(T[0][:, t * D:(t + 1) * D], h_a[:, kk * BW + t * P:kk * BW + (t + 1) * P],
                                              w_o[:, kk * D:(kk + 1) * D], start=kk == 0, stop=kk == KH - 1)
                mm.then_inc(s_fin, 1)

            TAIL3 = [(4, turn_sum), (11, turn_hn3), (14, h0), (17, lambda k: routed(k, 0)), (21, lambda k: routed(k, 1)),
                     (25, lambda k: routed(k, 2)), (29, lambda k: routed(k, 3)), (NT, out_proj)]

            def step3(k, slot, rnd, prev, nxt):
                pe.wait_ge(s_oT, k + 1)
                done = 0
                for n, piece in TAIL3:
                    if n > done:
                        mm = products3(k, slot, done, n)
                    if n == NT:
                        mm.then_inc(s_agg3, 1)
                    if prev:
                        piece(k)
                    done = n

            def last3(k):
                for n, piece in TAIL3:
                    piece(k)

            peeled(pe, step3, last3)


def kernel(**inputs):
    import numpy as _np
    import concourse.bacc as _bacc
    from concourse import mybir as _mybir
    from concourse.bass_utils import run_bass_kernel_spmd as _run

    g = {k: _np.asarray(v) for k, v in inputs.items()}

    def cols(M):
        return M.reshape(NT, P, NB, BW).transpose(2, 1, 0, 3).reshape(NB, P, NT * BW)

    def bc(v):
        return _np.broadcast_to(v.reshape(1, -1), (P, v.size))

    def by_part(W):
        return W.reshape(-1, P, W.shape[1]).transpose(1, 0, 2)

    def rep(v):
        return _np.broadcast_to(v.reshape(-1, P).T[:, :, None], (P, v.size // P, P)).reshape(P, -1)

    L = {
        "x": g["x"],
        "adj_cols": cols(g["adj"]),
        "adjT_cols": cols(g["adj"].T),
        "W_in1T": by_part(_np.ascontiguousarray(g["L0_gnn_W_in1"].T)).reshape(P, -1),
        "W_out1": by_part(g["L0_gnn_W_out1"]).reshape(P, -1),
        "W_in2T": g["L0_gnn_W_in2"].T,
        "W_out2": g["L0_gnn_W_out2"],
        "b_in1_rep": rep(g["L0_gnn_b_in1"]),
        "b_in2_rep": rep(g["L0_gnn_b_in2"]),
        "b_self1_bc": bc(g["L0_gnn_b_self1"]),
        "b_self2_bc": bc(g["L0_gnn_b_self2"]),
        "b_out1_bc": bc(g["L0_gnn_b_out1"]),
        "b_out2_bc": bc(g["L0_gnn_b_out2"]),
        "W_self1": g["L0_gnn_W_self1"],
        "W_self2": by_part(g["L0_gnn_W_self2"]),
        "gb1": _np.concatenate([g["L0_gnn_g1"].reshape(KH, P).T, g["L0_gnn_be1"].reshape(KH, P).T], axis=1),
        "gate_w": g["L0_ffn_gate_w"],
        "g2_bc": bc(g["L0_gnn_g2"]),
        "be2_bc": bc(g["L0_gnn_be2"]),
        "gate_b_bc": _np.tile(bc(g["L0_ffn_gate_b"]), (1, BT)),
        "w1": g["L0_ffn_w1"],
        "w2": g["L0_ffn_w2"].reshape(E1, FK, P, D).transpose(0, 2, 1, 3).reshape(E1, P, FK * D),
        "b1": g["L0_ffn_b1"].reshape(E1, FK, P).transpose(0, 2, 1),
        "b2_bc": _np.broadcast_to(g["L0_ffn_b2"][:, None, :], (E1, P, D)),
        "gnn_W": g["L1_gnn_W"].reshape(P, 1),
        "route": g["L1_ffn_route_id"].reshape(1, -1),
        "WiT": g["L1_ffn_Wi"].T,
        "bi": g["L1_ffn_bi"].reshape(KH, P).T,
        "Wr": g["L1_ffn_Wr"].reshape(L2, E2, DH, KH, P).transpose(0, 4, 1, 3, 2).reshape(L2, P, E2 * KH * DH),
        "br": g["L1_ffn_br"].reshape(L2, E2, KH, P).transpose(3, 0, 2, 1).reshape(P, L2 * KH * E2),
        "WsT": g["L1_ffn_Ws"].reshape(L2, DH, KH, P).transpose(3, 0, 2, 1).reshape(P, L2 * KH * DH),
        "bs": g["L1_ffn_bs"].reshape(L2, KH, P).transpose(2, 0, 1).reshape(P, L2 * KH),
        "WoT": by_part(_np.ascontiguousarray(g["L1_ffn_Wo"].T)).reshape(P, -1),
        "bo_bc": bc(g["L1_ffn_bo"]),
    }
    nc = _bacc.Bacc("TRN2", target_bir_lowering=False, num_devices=1)
    arrays, A = {}, {}
    for name, a in L.items():
        a = _np.ascontiguousarray(a)
        arrays[f"in_{name}"] = a
        A[name] = nc.dram_tensor(f"in_{name}", a.shape, _mybir.dt.from_np(a.dtype), kind="ExternalInput").ap()
    out = nc.dram_tensor("out_x", (N, D), F32, kind="ExternalOutput").ap()
    build(nc, A, out)
    r = _run(nc, [arrays], core_ids=[0])
    return r.results[0]["out_x"]
```

```python
from contextlib import ExitStack

import concourse.bass as bass
from concourse import mybir

F32 = mybir.dt.float32
BF16 = mybir.dt.bfloat16
I8 = mybir.dt.int8
I32 = mybir.dt.int32
U32 = mybir.dt.uint32
ALU = mybir.AluOpType
ACT = mybir.ActivationFunctionType
AX = mybir.AxisListType
ds = bass.ds

P = 128
N = 4096
D = 128
DH = 256
NT = N // P
BT = 4
BW = BT * P
NB = N // BW
HT = NT // 2
HALF = HT * BW
QT = NT // 4
QUART = QT * BW
E1 = 8
F1 = 512
FK = F1 // P
CAP = -(-5 * N // (4 * E1))
CT = CAP // P
EPARTS = ((0, 3), (3, CT))
CHUNKS = ((0, 4), (4, 8), (8, 12), (12, 18), (18, 24), (24, 32))
FIRST = 2
LN_DVE = 12
ROW = D + 2
E2 = 16
SEG = N // 64
SB = BW // SEG
KH = DH // P
L2 = 2
SH = SB // 2
NG = L2 * SB // SH

ORDER2 = (1, 2, 3, 0)
ROWS2 = [t for q in ORDER2[:3] for t in range(q * QT, (q + 1) * QT)] + list(range(BT, QT)) + list(range(BT))

THRESH = 1e-6
EPS = 1e-8
LN_EPS = 1e-5
SMALL = 2.0 ** -6
FMAX = 3.4028234e38
BIG = 1.0e4
NOWHERE = 1.0e6
CW = 2048
NC = HALF // CW


def build(nc, A, out):
    ctx = ExitStack()
    with ctx:
        def sb(name, shape, dt=F32):
            return ctx.enter_context(nc.sbuf_tensor(name, shape, dt))

        def pb(name, shape, dt=F32):
            return ctx.enter_context(nc.psum_tensor(name, shape, dt))

        def sem(name):
            return ctx.enter_context(nc.semaphore(name))

        thr_d = nc.dram_tensor("thr_d", [NB, BW], F32).ap()
        disp_d = nc.dram_tensor("disp_d", [E1 * CAP, ROW], F32).ap()
        y_d = nc.dram_tensor("y_d", [N, D], F32).ap()

        ring = [[sb(f"ring{s}{h}", [P, HALF]) for h in range(2)] for s in range(2)]
        S = sb("S", [P, NT * D])
        U = sb("U", [P, NT * D])
        R = sb("R", [P, NT * D])

        ident = sb("ident", [P, P])
        ones = sb("ones", [P, P])
        onesb = sb("onesb", [P, P], BF16)
        tri = sb("tri", [P, P], BF16)
        W_io = sb("W_io", [P, DH])
        W_s1 = sb("W_s1", [P, DH])
        W_us = sb("W_us", [P, KH, 2 * D])
        b_io = sb("b_io", [P, DH])
        b_all = sb("b_all", [P, DH])
        b_us = sb("b_us", [P, 2 * D])
        gb1 = sb("gb1", [P, 2 * KH])
        wgate = sb("wgate", [P, E1])
        rb = sb("rb", [P, NT])
        ne = sb("ne", [P, NT])
        neg_half = sb("neg_half", [P, 8])
        flags = sb("flags", [1, NB], I32)
        small = sb("small", [P, 96])
        sumc, rs_, ws_, rw_, nn = [small[:, 4 * i:4 * i + 4] for i in range(5)]
        rbp, cc = [[small[:, 72 + 8 * i + 4 * j:76 + 8 * i + 4 * j] for i in range(2)] for j in range(2)]
        smax, cdiff, bad1, bad = [small[:, 28 + i:29 + i] for i in range(4)]
        ve = small[:, 32:40]
        rstd = small[:, 40:48]
        csum = small[:, 48:48 + 2 * NC]
        cshift = small[:, 56:56 + 2 * NC]
        cmix = small[:, 64:64 + 2 * NC]
        st6 = sb("st6", [P, 8 * 6])
        mv = sb("mv", [P, 8 * 2])
        WORK = 22 * 256 + 64
        work = sb("work", [P, WORK])

        def part(at, n):
            return work[:, at:at + n]

        pA, thr, aT, hT, hs = [part(BW * i, BW) for i in range(5)]
        pre = [part(5 * BW + DH * i, DH) for i in range(2)]
        z1 = part(6 * BW, BT * DH)
        h1T = part(8 * BW, KH * BW)
        junk = part(10 * BW, CW // 4).bitcast(I8)
        p2T, xb, o2, hnT, msk = [part(BW * i, BW) for i in range(5)]
        thr2 = [part(BW * (5 + i), BW) for i in range(2)]
        rows = part(7 * BW, BT * ROW)
        at = 7 * BW + BT * ROW
        g2, be2 = part(at, D), part(at + D, D)
        at += 2 * D
        lg, ex, sc, cw, w8, cofs, gbc = [part(at + 32 * i, 32) for i in range(7)]
        at += 224
        lmax, esum, slot_f, tok = [part(at + 4 * i, 4) for i in range(4)]
        at += 16
        off = part(at, 5 * E1)
        at += 5 * E1
        idx = part(at, BT).bitcast(U32)
        at += 4
        oh = part(at, 16).bitcast(BF16)
        at += 16
        rb4 = part(at, 4)
        assert at + 4 <= WORK

        at = 0
        e_rows = [part(at + CT * ROW * i, CT * ROW) for i in range(2)]
        at += 2 * CT * ROW
        e_w1 = [part(at + F1 * i, F1) for i in range(2)]
        at += 2 * F1
        e_w2 = [part(at + F1 * i, FK * D) for i in range(2)]
        at += 2 * FK * D
        e_b2 = [part(at + D * i, D) for i in range(2)]
        at += 2 * D
        e_b1 = [part(at + FK * i, FK) for i in range(2)]
        at += 2 * FK
        e_idx = [part(at + 8 * i, CT).bitcast(U32) for i in range(2)]
        at += 16
        e_xT = U[:, 0:CAP]
        e_hm = U[:, CAP:(1 + FK) * CAP]
        e_y = [R[:, CAP * i:CAP * (i + 1)] for i in range(2)]
        e_fin, e_pos, e_neg = [R[:, CAP * (2 + i):CAP * (3 + i)] for i in range(3)]
        e_prob = [R[:, CAP * 5 + 8 * i:CAP * 5 + 8 * i + CT] for i in range(2)]
        w_i = part(at, DH)
        at += DH
        w_s = part(at, L2 * KH * DH)
        at += L2 * KH * DH
        w_o = part(at, KH * D)
        at += KH * D
        b_o = part(at, D)
        at += D
        b_i = part(at, KH)
        b_r = part(at + KH, L2 * KH * E2)
        at += KH + L2 * KH * E2
        b_s = part(at, L2 * KH)
        w_g = part(at + L2 * KH, 1)
        at += L2 * KH + 1
        route_sb = part(at, N // SEG)[0:1].bitcast(I32)
        assert at + N // SEG <= WORK
        F2_INPUTS = [(w_i, "WiT"), (w_s, "WsT"), (w_o, "WoT"), (b_o, "bo_bc"), (b_i, "bi"), (b_r, "br"), (b_s, "bs"),
                     (w_g, "gnn_W"), (route_sb[:, :], "route")]
        oT, x3, hn3, hT3, ob = [part(BW * i, BW) for i in range(5)]
        h_b = part(5 * BW, KH * BW)
        assert 7 * BW <= 2 * CT * ROW + 2 * F1 + 2 * FK * D + 2 * D + 2 * FK + 16
        h_a = U[:, 0:KH * BW]
        WS = 4
        wst = [U[:, KH * BW + KH * DH * i:KH * BW + KH * DH * (i + 1)] for i in range(WS)]

        mv3 = e_rows[0][:, 0:2 * NT]
        rstd3, nm3, ve3 = [e_rows[0][:, NT * i:NT * (i + 1)] for i in range(2, 5)]

        def tiles(ap, n=BT, w=D):
            return ap.rearrange("p (t d) -> p t d", t=n, d=w)

        fill = R[:, 0:10 * ROW]
        t_at = 1408
        t_in1T = R[:, t_at:t_at + 256]
        t_out1 = R[:, t_at + 256:t_at + 768]
        t_in2T = R[:, t_at + 768:t_at + 1024]
        t_out2 = R[:, t_at + 1024:t_at + 1152]
        t_bin1 = R[:, t_at + 1152:t_at + 1408]
        t_bin2 = R[:, t_at + 1408:t_at + 1536]
        t_bs1 = R[:, t_at + 1536:t_at + 1792]
        t_bs2 = R[:, t_at + 1792:t_at + 1920]

        WEIGHTS = ((t_in1T, "W_in1T"), (t_out1, "W_out1"), (t_in2T, "W_in2T"), (t_out2, "W_out2"),
                   (t_bin1, "b_in1_rep"), (t_bin2, "b_in2_rep"), (t_bs1, "b_self1_bc"), (t_bs2, "b_self2_bc"),
                   (b_all[:, :], "b_out1_bc"), (b_us[:, D:2 * D], "b_out2_bc"), (W_s1[:, :], "W_self1"),
                   (W_us[:, :, D:2 * D], "W_self2"), (gb1[:, :], "gb1"), (wgate[:, :], "gate_w"))
        zeros = R[:, t_at + 1920:t_at + 1920 + BW]
        NZ = N * D // (P * BW)
        FILLED = 16 * (NZ + 4)
        mv0, rstd0, ve0, st0 = z1[:, 0:2 * NT], z1[:, 2 * NT:3 * NT], z1[:, 3 * NT:4 * NT], z1[:, 4 * NT:10 * NT]

        PA = [pb(f"PA{i}", [P, BW]) for i in range(2)]
        SR = pb("SR", [P, BW])
        SM = pb("SM", [P, BW])
        T = [pb(f"T{i}", [P, BW]) for i in range(2)]
        O = [pb(f"O{i}", [P, BW]) for i in range(2)]
        HB = [PA[0], PA[1], SR, SM]
        LB = [SR, SM, O[0], O[1]]

        s_wts = sem("s_wts")
        s_wts2 = sem("s_wts2")
        s_xin = [sem(f"s_xin{c}") for c in range(4)]
        s_ring = [[sem(f"s_ring{s}{q}") for q in range(4)] for s in range(2)]
        s_const = sem("s_const")
        s_zero = sem("s_zero")
        s_fill = sem("s_fill")
        s_wprod = sem("s_wprod")
        s_wready = sem("s_wready")
        s_mv0 = sem("s_mv0")
        s_rstd0 = sem("s_rstd0")
        s_hn = sem("s_hn")
        s_ms = sem("s_ms")
        s_msp = sem("s_msp")
        s_part = sem("s_part")
        s_sums = sem("s_sums")
        s_thr = sem("s_thr")
        s_thrst = sem("s_thrst")
        s_cnt = sem("s_cnt")
        s_bad = sem("s_bad")
        s_flag = sem("s_flag")
        s_clean = sem("s_clean")
        s_quart = sem("s_quart")
        s_agg = sem("s_agg")
        s_aT = sem("s_aT")
        s_neh = sem("s_neh")
        s_hs = sem("s_hs")
        s_hTp = sem("s_hTp")
        s_hT = sem("s_hT")
        s_o1 = sem("s_o1")
        s_o1u = sem("s_o1u")
        s_pre = sem("s_pre")
        s_mv = sem("s_mv")
        s_rstd = sem("s_rstd")
        s_ve = sem("s_ve")
        s_own = sem("s_own")
        s_z = sem("s_z")
        s_zT = sem("s_zT")
        s_h1T = sem("s_h1T")
        s_u2 = sem("s_u2")
        s_u2u = sem("s_u2u")
        s_thr2 = [sem(f"s_thr2{i}") for i in range(2)]
        s_clean2 = sem("s_clean2")
        s_quart2 = sem("s_quart2")
        s_agg2 = sem("s_agg2")
        s_p2 = sem("s_p2")
        s_t2 = sem("s_t2")
        s_t2u = sem("s_t2u")
        s_mv2 = sem("s_mv2")
        s_rstd2 = sem("s_rstd2")
        s_xb = sem("s_xb")
        s_x1 = sem("s_x1")
        s_hn2 = sem("s_hn2")
        s_hn2p = sem("s_hn2p")
        s_hn2T = sem("s_hn2T")
        s_lg = sem("s_lg")
        s_l2 = sem("s_l2")
        s_ex = sem("s_ex")
        s_oh = sem("s_oh")
        s_cum = sem("s_cum")
        s_idx = sem("s_idx")
        s_sc = sem("s_sc")
        s_rin = [sem(f"s_rin{i}") for i in range(2)]
        s_ein = [sem(f"s_ein{i}") for i in range(2)]
        s_xTp = sem("s_xTp")
        s_xT = sem("s_xT")
        s_h1 = sem("s_h1")
        s_hm = sem("s_hm")
        s_yp = sem("s_yp")
        s_ye = sem("s_ye")
        s_y = sem("s_y")
        s_sc2 = [sem(f"s_sc2{i}") for i in range(2)]
        s_wts3 = sem("s_wts3")
        s_yin = [sem(f"s_yin{c}") for c in range(len(CHUNKS))]
        s_mv3 = sem("s_mv3")
        s_rstd3 = sem("s_rstd3")
        s_hid = sem("s_hid")
        s_hid2 = sem("s_hid2")
        s_quart3 = sem("s_quart3")
        s_agg3 = sem("s_agg3")
        s_oT = sem("s_oT")
        s_oTt = sem("s_oTt")
        s_x3 = sem("s_x3")
        s_mv4 = sem("s_mv4")
        s_rstd4 = sem("s_rstd4")
        s_hn3 = sem("s_hn3")
        s_hn3p = sem("s_hn3p")
        s_hT3 = sem("s_hT3")
        s_h0p = sem("s_h0p")
        s_h0 = sem("s_h0")
        s_wst = sem("s_wst")
        s_wu = sem("s_wu")
        s_l = sem("s_l")
        s_fin = sem("s_fin")
        s_x3b = sem("s_x3b")
        s_out = sem("s_out")
        s_stored = sem("s_stored")
        s_fin2 = sem("s_fin2")

        def load_quarter(eng, M, b, slot, q):
            at = q % 2 * QUART
            eng.dma_start(ring[slot][q // 2][:, at:at + QUART],
                          M[ds(b, 1), :, q * QUART:(q + 1) * QUART].rearrange("o p n -> (o p) n")).then_inc(s_ring[slot][q], 16)

        def peeled(eng, step, drain):
            step(0, 0, 0, False, True)
            with eng.Fori(0, NB // 2 - 1) as i:
                step(i * 2 + 1, 1, i, True, True)
                step(i * 2 + 2, 0, i + 1, True, True)
            step(NB - 1, 1, NB // 2 - 1, True, False)
            drain(NB)

        def peeled1(eng, step):
            def at(k):
                step(k, k % 2, k // 2, {d: 0 <= k + d < NB for d in (-2, -1, 1, 2)})
            at(0)
            at(1)
            with eng.Fori(1, NB // 2 - 1) as i:
                for par in range(2):
                    step(i * 2 + par, par, i, {-2: True, -1: True, 1: True, 2: True})
            at(NB - 2)
            at(NB - 1)

        def scan(eng, k):
            return (NB - 1) - k

        ticks = {nc.sync: sem("tick_sp"), nc.scalar: sem("tick_act"), nc.gpsimd: sem("tick_pool"), nc.vector: sem("tick_dve")}

        def alone(eng):
            eng.sem_inc(ticks[eng], 1)

        adjc, adjT = A["adj_cols"], A["adjT_cols"]
        x_t = A["x"].rearrange("(t p) d -> p t d", p=P)
        disp_t = disp_d.rearrange("(t p) r -> p t r", p=P)
        y_t = y_d.rearrange("(t p) d -> p t d", p=P)
        out_t = out.rearrange("(t p) d -> p t d", p=P)
        block = ctx.enter_context(nc.Block())

        @block.sync
        def _(sp):
            load_quarter(sp, adjc, scan(sp, 0), 0, 0)
            for c in range(4):
                sp.dma_start(tiles(S[:, c * 1024:(c + 1) * 1024], 8), x_t[:, 8 * c:8 * c + 8, :]).then_inc(s_xin[c], 16)
            for q in range(1, 4):
                load_quarter(sp, adjc, scan(sp, 0), 0, q)
            for dst, name in WEIGHTS:
                sp.dma_start(dst, A[name]).then_inc(s_wts, 16)
            for q in range(2):
                load_quarter(sp, adjc, scan(sp, 1), 1, q)
            sp.wait_ge(s_thrst, 16)
            for q in range(2, 4):
                load_quarter(sp, adjc, scan(sp, 1), 1, q)

            def store_thr(k):
                sp.wait_ge(s_thr, k + 1)
                alone(sp)
                sp.dma_start(thr_d[ds(scan(sp, k), 1), :], thr[0:1, :]).then_inc(s_thrst, 16)

            def refill(k, slot):
                for q in range(3):
                    sp.wait_ge(s_quart, (k - 2) * 3 + q + 1)
                    alone(sp)
                    load_quarter(sp, adjc, scan(sp, k), slot, q)
                store_thr(k - 1)
                sp.wait_ge(s_agg, k - 1)
                alone(sp)
                load_quarter(sp, adjc, scan(sp, k), slot, 3)

            refill(2, 0)
            sp.wait_ge(s_zero, 1)
            y_rows = y_d.rearrange("(p t) d -> p (t d)", p=P)
            for q in range(NZ):
                sp.dma_start(y_rows[:, q * BW:(q + 1) * BW], zeros).then_inc(s_fill, 16)
            for q in range(4):
                n = E1 * CAP // 4
                sp.dma_start(disp_d[q * n:(q + 1) * n, :].rearrange("(p t) r -> p (t r)", p=P), fill).then_inc(s_fill, 16)
            refill(3, 1)
            with sp.Fori(1, NB // 2 - 1) as i:
                refill(i * 2 + 2, 0)
                refill(i * 2 + 3, 1)
            store_thr(NB - 1)
            sp.wait_ge(s_thrst, 16 * NB)

            def block_inputs(j, slot):
                sp.wait_ge(s_clean2, j - 1)
                alone(sp)
                sp.dma_start(thr2[slot][:, :], thr_d[ds(j, 1), :].to_broadcast([P, BW])).then_inc(s_thr2[slot], 16)

            def load_xb(j):
                sp.wait_ge(s_x1, j + 1)
                alone(sp)
                sp.dma_start(tiles(xb), x_t[:, ds(j * BT, BT), :]).then_inc(s_xb, 16)

            def tail_inputs():
                sp.wait_ge(s_u2u, 2 + 2 * NB)
                sp.wait_ge(s_own, NB)
                sp.dma_start(g2, A["g2_bc"]).then_inc(s_wts2, 16)
                sp.dma_start(be2, A["be2_bc"]).then_inc(s_wts2, 16)
                sp.dma_start(gbc, A["gate_b_bc"]).then_inc(s_wts2, 16)

            def refill2(j, slot):
                for n, q in enumerate(ORDER2):
                    if n < 3:
                        sp.wait_ge(s_quart2, (j - 2) * 3 + n + 1)
                    else:
                        sp.wait_ge(s_agg2, j - 1)
                    alone(sp)
                    load_quarter(sp, adjc, j, slot, q)
                    if n == 1:
                        if isinstance(j, int) and j == 2:
                            tail_inputs()
                        load_xb(j - 2)
                block_inputs(j, slot)

            refill2(2, 1)
            refill2(3, 0)
            with sp.Fori(1, NB // 2 - 1) as i:
                refill2(i * 2 + 2, 1)
                refill2(i * 2 + 3, 0)
            load_xb(NB - 2)

            for n, q in enumerate(ORDER2):
                if n < 3:
                    sp.wait_ge(s_quart2, (NB - 2) * 3 + n + 1)
                else:
                    sp.wait_ge(s_agg2, NB - 1)
                load_quarter(sp, adjT, 0, 1, q)
            load_xb(NB - 1)
            sp.wait_ge(s_agg2, NB)
            sp.wait_ge(s_sc, 16 * (NT - BT))
            sp.dma_start(ring[0][0][:, :], A["Wr"][0]).then_inc(s_ring[0][0], 16)
            sp.dma_start(ring[0][1][:, 0:QUART], A["Wr"][1, :, 0:QUART]).then_inc(s_ring[0][2], 16)
            sp.wait_ge(s_sc, 16 * NT)

            def load_expert(e, par):
                if not isinstance(e, int):
                    sp.wait_ge(s_ye, e)
                    alone(sp)
                sp.dma_start(tiles(e_rows[par], CT, ROW), disp_t[:, ds(e * CT, CT), :]).then_inc(s_rin[par], 16)
                sp.dma_start(e_w1[par], A["w1"][ds(e, 1)].rearrange("o p f -> (o p) f")).then_inc(s_ein[par], 16)
                sp.dma_start(e_w2[par], A["w2"][ds(e, 1)].rearrange("o p f -> (o p) f")).then_inc(s_ein[par], 16)
                sp.dma_start(e_b1[par], A["b1"][ds(e, 1)].rearrange("o p f -> (o p) f")).then_inc(s_ein[par], 16)
                sp.dma_start(e_b2[par], A["b2_bc"][ds(e, 1)].rearrange("o p f -> (o p) f")).then_inc(s_ein[par], 16)

            load_expert(0, 0)
            load_expert(1, 1)
            sp.dma_start(ring[0][1][:, QUART:HALF], A["Wr"][1, :, QUART:HALF]).then_inc(s_ring[0][3], 16)
            for dst, name in F2_INPUTS:
                sp.dma_start(dst, A[name]).then_inc(s_wts3, 16)
            with sp.Fori(1, E1 // 2) as i:
                load_expert(i * 2, 0)
                load_expert(i * 2 + 1, 1)

            for par in range(2):
                sp.wait_ge(s_sc2[par], 16 * CT * E1 // 2)
            for c, (lo, hi) in enumerate(CHUNKS):
                sp.dma_start(tiles(R[:, lo * D:hi * D], hi - lo), y_t[:, lo:hi, :]).then_inc(s_yin[c], 16)

            with sp.Fori(1, NB) as b:
                for q in range(4):
                    if q < 3:
                        sp.wait_ge(s_quart3, (b - 1) * 3 + q + 1)
                    else:
                        sp.wait_ge(s_agg3, b)
                    alone(sp)
                    load_quarter(sp, adjT, b, 1, q)
            sp.wait_ge(s_stored, 16 * NB)

        @block.scalar
        def _(act):
            def check(k, slot, rnd):
                act.wait_ge(s_bad, k + 1)
                alone(act)
                for col in range(2 * NC):
                    if col % (NC // 2) == 0:
                        act.wait_ge(s_ring[slot][col // (NC // 2)], (rnd + 1) * 16)
                        alone(act)
                    src = ring[slot][col // NC][:, col % NC * CW:(col % NC + 1) * CW]
                    act.drain()
                    nc.scalar.activation(junk, src, ACT.Sign, accum_out=csum[:, col:col + 1])
                    act.drain()
                    last = nc.scalar.activation(junk, src, ACT.Sign, bias=neg_small[:, 0:1], accum_out=cshift[:, col:col + 1])
                last.then_inc(s_cnt, 1)

            neg_small = neg_half[:, 7:8]
            act.wait_ge(s_const, 1)
            check(0, 0, 0)
            act.wait_ge(s_thr, 1)
            act.dma_start(thr_d[NB - 1:NB, :], thr[0:1, :]).then_inc(s_thrst, 16)
            act.wait_ge(s_wts, 16 * len(WEIGHTS))

            def evac_hT(k):
                act.wait_ge(s_hTp, k + 2)
                nc.scalar.copy(hT, T[0][:, :]).then_inc(s_hT, 1)

            def relu_h1(k):
                act.wait_ge(s_zT, k)
                for f in range(KH):
                    last = nc.scalar.activation(h1T[:, f * BW:(f + 1) * BW], T[f][:, :], ACT.Relu,
                                                bias=gb1[:, KH + f:KH + f + 1], scale=gb1[:, f:f + 1])
                last.then_inc(s_h1T, 1)

            def step(k, slot, rnd, has):
                if has[1]:
                    check(k + 1, 1 - slot, rnd + slot)
                if has[-1]:
                    relu_h1(k)
                evac_hT(k)

            peeled1(act, step)
            relu_h1(NB)

            def step2(k, slot, rnd, prev, nxt):
                if not prev:
                    return
                act.wait_ge(s_agg2, k)
                act.wait_ge(s_t2, k)
                nc.scalar.copy(p2T, PA[1 - slot][:, :]).then_inc(s_p2, 1)
                act.wait_ge(s_hn2p, k)
                nc.scalar.copy(hnT, T[1][:, :]).then_inc(s_hn2T, 1)
                act.wait_ge(s_l2, k)
                nc.scalar.activation(ex, lg, ACT.Exp).then_inc(s_ex, 1)

            peeled(act, step2, lambda k: step2(k, 0, 0, True, False))

            def expert(e, par):
                act.wait_ge(s_xTp, e + 1)
                nc.scalar.copy(e_xT[:, 0:BW], T[0][:, :])
                nc.scalar.copy(e_xT[:, BW:CAP], T[1][:, 0:CAP - BW]).then_inc(s_xT, 1)
                for q in range(2 * FK):
                    f, c = q // 2, q % 2
                    act.wait_ge(s_h1, e * (2 * FK) + q + 1)
                    nc.scalar.activation(e_hm[:, f * CAP + c * CAP // 2:f * CAP + (c + 1) * CAP // 2], HB[q % 4][:, 0:CAP // 2],
                                         ACT.Relu, bias=e_b1[par][:, f:f + 1]).then_inc(s_hm, 1)

            with act.Fori(0, E1 // 2) as i:
                for par in range(2):
                    act.wait_ge(s_ein[par], (i + 1) * 64)
                    expert(i * 2 + par, par)

            act.wait_ge(s_wts3, 16 * len(F2_INPUTS))
            act.wait_ge(s_fin2, 1)
            for c, (lo, hi) in enumerate(CHUNKS):
                if c >= FIRST:
                    act.wait_ge(s_rstd3, c + 1)
                    for t in range(lo, hi):
                        nc.scalar.activation(S[:, t * D:(t + 1) * D], R[:, t * D:(t + 1) * D], ACT.Identity, bias=nm3[:, t:t + 1])
                    act.drain()
                    for t in range(lo, hi):
                        last = nc.scalar.activation(S[:, t * D:(t + 1) * D], S[:, t * D:(t + 1) * D], ACT.Copy, scale=rstd3[:, t:t + 1])
                    last.then_inc(s_hid2, 1)

            def step3(k, slot, rnd, prev, nxt):
                if not prev:
                    return
                act.wait_ge(s_agg3, k)
                act.wait_ge(s_oTt, k)
                nc.scalar.activation(oT, PA[1 - slot][:, :], ACT.Copy, scale=w_g[:, 0:1]).then_inc(s_oT, 1)
                act.wait_ge(s_hn3p, k)
                nc.scalar.copy(hT3, T[1][:, :]).then_inc(s_hT3, 1)
                act.wait_ge(s_h0p, k)
                for m in range(KH):
                    last = nc.scalar.activation(h_a[:, m * BW:(m + 1) * BW], O[m][:, :], ACT.Relu, bias=b_i[:, m:m + 1])
                last.then_inc(s_h0, 1)
                for n in range(L2 * SB):
                    l, s = n // SB, n % SB
                    dst = (h_b, h_a)[l]
                    if s % SH == 0:
                        act.wait_ge(s_wu, (k - 1) * (L2 * SB) + n + SH + WS)
                        alone(act)
                    e = act.value_load(route_sb[0:1, ds((k - 1) * SB + s, 1)], min_val=0, max_val=E2 - 1)
                    for m in range(KH):
                        at = m * SH * SEG + s % SH * SEG
                        last = nc.scalar.activation(dst[:, m * BW + s * SEG:m * BW + (s + 1) * SEG], LB[n // SH][:, at:at + SEG],
                                                    ACT.Relu, bias=b_r[:, ds(e + (l * KH + m) * E2, 1)])
                    if s % SH == SH - 1:
                        last.then_inc(s_l, 1)

            peeled(act, step3, lambda k: step3(k, 0, 0, True, False))

        @block.gpsimd
        def _(pool):
            nc.gpsimd.memset(ident[:, :], 0.0)
            nc.gpsimd.memset(onesb[:, :], 1.0)
            nc.gpsimd.memset(ones[:, :], 1.0)
            nc.gpsimd.memset(neg_half[:, 0:7], -0.5)
            pool.drain()
            nc.gpsimd.memset(neg_half[:, 7:8], -SMALL)
            nc.gpsimd.affine_select(out=ident[:, :], in_=ident[:, :], compare_op=ALU.not_equal, fill=1.0, base=0,
                                    pattern=[[-1, P]], channel_multiplier=1)
            nc.gpsimd.affine_select(out=tri[:, :], in_=onesb[:, :], compare_op=ALU.is_ge, fill=0.0, base=0,
                                    pattern=[[1, P]], channel_multiplier=-1).then_inc(s_const, 1)
            nc.gpsimd.memset(zeros, 0.0)
            nc.gpsimd.memset(fill, 0.0)
            pool.drain()
            nc.gpsimd.memset(tiles(fill, 10, ROW)[:, :, D + 1], NOWHERE).then_inc(s_zero, 1)

            def inv_sqrt(n, var, s_in, at_in, s_out, nth, ve=ve, rstd=rstd):
                pool.wait_ge(s_in, at_in)
                alone(pool)
                nc.gpsimd.tensor_scalar(ve[:, 0:n], var, LN_EPS, 0.0, ALU.add, ALU.add).then_inc(s_ve, 1)
                pool.wait_ge(s_ve, nth)
                alone(pool)
                nc.gpsimd.tensor_tensor(rstd[:, 0:n], ve[:, 0:n], neg_half[:, 0:1].to_broadcast([P, n]), ALU.pow).then_inc(s_out, 1)

            mv8 = tiles(mv[:, :], 8, 2)
            inv_sqrt(NT, tiles(mv0, NT, 2)[:, :, 1], s_mv0, 1, s_rstd0, 1, ve0, rstd0)
            pool.wait_ge(s_rstd0, 1)
            for t in range(LN_DVE, NT):
                tile = S[:, t * D:(t + 1) * D]
                last = nc.gpsimd.tensor_scalar(tile, tile, mv0[:, 2 * t:2 * t + 1], rstd0[:, t:t + 1], ALU.subtract, ALU.mult)
            last.then_inc(s_hn, 1)

            def stage(k):
                pool.wait_ge(s_hTp, k + 1)
                alone(pool)
                nc.gpsimd.tensor_copy(hs, S[:, ds(scan(pool, k) * BW, BW)]).then_inc(s_hs, 1)

            def bias_rows(kk, slot):
                pool.wait_ge(s_msp, kk + 1)
                alone(pool)
                for t in range(BT):
                    pool.wait_ge(s_o1u, kk * BT + t + 1)
                    alone(pool)
                    nc.gpsimd.tensor_scalar(pre[t % 2], b_io[:, :], cc[slot][:, t:t + 1], None, ALU.mult)
                    pool.drain()
                    nc.gpsimd.tensor_tensor(pre[t % 2], pre[t % 2], b_all[:, :], ALU.add).then_inc(s_pre, 1)

            def own_T2(kk):
                blk = scan(pool, kk)
                pool.wait_ge(s_u2u, kk * 2 + 4)
                alone(pool)
                cols = ds(blk * BW, BW)
                nc.gpsimd.tensor_tensor(tiles(z1[:, 0:BW]), tiles(U[:, cols]), ne[:, ds(blk * BT, BT)].unsqueeze(2).to_broadcast([P, BT, D]), ALU.mult)
                pool.drain()
                nc.gpsimd.tensor_tensor(R[:, cols], R[:, cols], z1[:, 0:BW], ALU.add).then_inc(s_own, 1)
                pool.drain()

            def step(k, slot, rnd, has):
                stage(k)
                if has[-2]:
                    own_T2(k - 2)
                if has[-1]:
                    bias_rows(k - 1, 1 - slot)
                    inv_sqrt(BT, mv8[:, 0:BT, 1], s_mv, k, s_rstd, k + 1)
                pool.wait_ge(s_msp, k + 1)
                alone(pool)
                pool.wait_ge(s_hT, k + 1)
                alone(pool)
                cols = ds(scan(pool, k) * BW, BW)
                nc.gpsimd.tensor_tensor(U[:, cols], U[:, cols], hT, ALU.mult).then_inc(s_neh, 1)

            pool.wait_ge(s_hn, 2)
            pool.wait_ge(s_wready, 1)
            peeled1(pool, step)
            own_T2(NB - 2)
            bias_rows(NB - 1, 1)
            inv_sqrt(BT, mv8[:, 0:BT, 1], s_mv, NB, s_rstd, NB + 1)
            own_T2(NB - 1)

            pool.wait_ge(s_u2u, 2 + 2 * NB)
            nc.gpsimd.iota(w8, pattern=[[0, BT], [-1, E1]], base=E1, channel_multiplier=0, allow_small_or_imprecise_dtypes=True)
            nc.gpsimd.iota(cofs, pattern=[[0, BT], [CAP, E1]], base=-1, channel_multiplier=0, allow_small_or_imprecise_dtypes=True)
            nc.gpsimd.iota(tok, pattern=[[P, BT]], base=0, channel_multiplier=1, allow_small_or_imprecise_dtypes=True)
            nc.gpsimd.memset(off[:, 0:E1], 0.0).then_inc(s_const, 1)
            pool.wait_ge(s_fill, FILLED)

            def step2(k, slot, rnd, prev, nxt):
                if not prev:
                    return
                inv_sqrt(BT, mv8[:, 0:BT, 1], s_mv2, k * 2 - 1, s_rstd2, k * 2 + 8)
                inv_sqrt(BT, mv8[:, 0:BT, 1], s_mv2, k * 2, s_rstd2, k * 2 + 9)
                pool.wait_ge(s_idx, k)
                alone(pool)
                for t in range(BT):
                    nc.gpsimd.indirect_dma_start(disp_d, bass.IndirectOffsetOnAxis(ap=idx[:, t:t + 1], axis=0),
                                                 rows[:, t * ROW:(t + 1) * ROW], None,
                                                 bounds_check=E1 * CAP - 1, oob_is_err=False).then_inc(s_sc, 16)

            peeled(pool, step2, lambda k: step2(k, 0, 0, True, False))

            with pool.Fori(0, E1 // 2) as i:
                for par in range(2):
                    for n, (lo, hi) in enumerate(EPARTS):
                        pool.wait_ge(s_y, i * 4 + par * 2 + n + 1)
                        alone(pool)
                        for q in range(lo, hi):
                            nc.gpsimd.indirect_dma_start(y_d, bass.IndirectOffsetOnAxis(ap=e_idx[par][:, q:q + 1], axis=0),
                                                         e_y[par][:, q * D:(q + 1) * D], None,
                                                         bounds_check=N - 1, oob_is_err=False).then_inc(s_sc2[par], 16)
            for c, (lo, hi) in enumerate(CHUNKS):
                if c >= FIRST:
                    pool.wait_ge(s_mv3, c + 1)
                    nc.gpsimd.tensor_scalar(nm3[:, lo:hi], tiles(mv3, NT, 2)[:, lo:hi, 0], -1.0, 0.0, ALU.mult, ALU.add)
                inv_sqrt(hi - lo, tiles(mv3, NT, 2)[:, lo:hi, 1], s_mv3, c + 1, s_rstd3, c + 26, ve3[:, lo:hi], rstd3[:, lo:hi])

            def step3(k, slot, rnd, prev, nxt):
                if not prev:
                    return
                inv_sqrt(BT, mv8[:, 0:BT, 1], s_mv4, k, s_rstd4, k + 25 + len(CHUNKS))
                pool.wait_ge(s_hn3, k)
                alone(pool)
                nc.gpsimd.tensor_tensor(tiles(x3), tiles(x3), b_o.unsqueeze(1).to_broadcast([P, BT, D]), ALU.add).then_inc(s_x3b, 1)
                pool.wait_ge(s_out, k + 1)
                alone(pool)
                nc.gpsimd.dma_start(out_t[:, ds((k - 1) * BT, BT), :], tiles(ob)).then_inc(s_stored, 16)

            peeled(pool, step3, lambda k: step3(k, 0, 0, True, False))

        @block.vector
        def _(dve):
            mv8 = tiles(mv[:, :], 8, 2)

            def stats(tile_of, n):
                for t in range(n):
                    nc.vector.bn_stats(st6[:, 6 * t:6 * t + 6], tile_of(t))
                dve.drain()
                for t in range(n):
                    last = nc.vector.bn_aggr(mv8[:, t, :], st6[:, 6 * t:6 * t + 6])
                return last

            nc.vector.memset(small[:, 28:32], 0.0).then_inc(s_aT, 2)
            nc.vector.memset(sumc, 0.0).then_inc(s_o1u, 2)
            nc.vector.memset(rbp[0], 0.0).then_inc(s_u2u, 2)
            nc.vector.memset(cc[0], 0.0).then_inc(s_hTp, 1)
            nc.vector.memset(rs_, 0.0).then_inc(s_bad, 1)
            nc.vector.memset(ws_, 0.0).then_inc(s_p2, 2)
            nc.vector.memset(nn, 0.0).then_inc(s_t2, 1)
            nc.vector.memset(small[:, 24:26], 0.0).then_inc(s_t2u, 1)
            nc.vector.memset(small[:, 20:24], 0.0).then_inc(s_clean2, 2)
            nc.vector.memset(rw_, 0.0).then_inc(s_x1, 1)
            for c in range(4):
                dve.wait_ge(s_xin[c], 16)
                for t in range(8 * c, 8 * c + 8):
                    nc.vector.bn_stats(st0[:, 6 * t:6 * t + 6], S[:, t * D:(t + 1) * D])
            dve.drain()
            for t in range(NT):
                last = nc.vector.bn_aggr(mv0[:, 2 * t:2 * t + 2], st0[:, 6 * t:6 * t + 6])
            last.then_inc(s_mv0, 1)

            def reduce_half(dst, slot, h):
                nc.vector.tensor_reduce(dst, ring[slot][h].rearrange("p (t c) -> p c t", t=HT, c=BW), AX.X, ALU.add)

            def sum_halves():
                dve.drain()
                nc.vector.tensor_tensor(pA, pA, thr, ALU.add).then_inc(s_part, 1)

            def partials(k, slot, rnd, h):
                if not isinstance(k, int) or k > 0:
                    if h == 0:
                        dve.wait_ge(s_thrst, k * 16)
                    else:
                        dve.wait_ge(s_ms, k)
                    alone(dve)
                for q in range(2 * h, 2 * h + 2):
                    dve.wait_ge(s_ring[slot][q], (rnd + 1) * 16)
                    alone(dve)
                reduce_half((thr, pA)[h], slot, h)

            def mask_block(slot, th, tmp):
                for h in range(2):
                    with dve.Fori(0, HT) as t:
                        piece = ring[slot][h][:, ds(t * BW, BW)]
                        nc.vector.tensor_tensor(tmp, piece, th, ALU.is_gt)
                        dve.drain()
                        nc.vector.tensor_tensor(piece, piece, tmp, ALU.mult)
                        dve.drain()

            def thresholds(k):
                dve.wait_ge(s_sums, k + 1)
                alone(dve)
                nc.vector.tensor_scalar(thr, SR[:, :], EPS, THRESH, ALU.add, ALU.mult)
                nc.vector.tensor_scalar(sumc, SM[:, 0:BT], EPS, None, ALU.add)
                dve.drain()
                nc.vector.tensor_reduce(smax, thr, AX.X, ALU.max).then_inc(s_thr, 1)

            def verdict(k):
                dve.wait_ge(s_cnt, k + 1)
                alone(dve)
                nc.vector.scalar_tensor_tensor(cmix, csum, -2.0, cshift, ALU.mult, ALU.add, accum_out=cdiff)
                dve.drain()
                nc.vector.tensor_scalar(bad1, cdiff, float(-2 * HALF), None, ALU.not_equal)
                dve.drain()
                nc.vector.scalar_tensor_tensor(bad, smax, SMALL, bad1, ALU.is_ge, ALU.add).then_inc(s_bad, 1)

            def mask_if_needed(k, slot):
                blk = scan(dve, k)
                dve.wait_ge(s_flag, k + 1)
                alone(dve)
                nc.vector.tensor_copy(flags[0:1, ds(blk, 1)], SM[0:1, 2 * BT:2 * BT + 1])
                dve.drain()
                flag = dve.value_load(flags[0:1, ds(blk, 1)], min_val=0, max_val=2 * P)
                with dve.If(flag > 0):
                    mask_block(slot, thr, pA)
                    reduce_half(pA, slot, 0)
                    dve.wait_ge(s_thrst, k * 16 + 16)
                    alone(dve)
                    reduce_half(thr, slot, 1)
                    dve.drain()
                    nc.vector.tensor_tensor(pA, pA, thr, ALU.add)
                    dve.drain()
                dve.drain().then_inc(s_clean, 1)

            def scales(k, slot):
                blk = scan(dve, k)
                dve.wait_ge(s_ms, k + 1)
                alone(dve)
                ms = SM[:, BT:2 * BT]
                nc.vector.tensor_scalar(U[:, ds(blk * BW, BW)], SR[:, :], 0.0, None, ALU.is_le)
                nc.vector.reciprocal(rs_, sumc)
                nc.vector.tensor_scalar(nn, ms, 0.0, None, ALU.is_gt)
                nc.vector.tensor_scalar(ne[:, ds(blk * BT, BT)], ms, 0.0, None, ALU.is_le)
                nc.vector.tensor_scalar(cc[slot], ms, 0.0, None, ALU.is_le)
                dve.drain()
                nc.vector.tensor_tensor(ws_, ms, rs_, ALU.mult)
                dve.drain()
                nc.vector.tensor_scalar(rw_, ws_, EPS, None, ALU.add)
                dve.drain()
                nc.vector.reciprocal(rw_, rw_)
                dve.drain()
                nc.vector.tensor_tensor(rs_, rs_, rw_, ALU.mult)
                nc.vector.tensor_tensor(ws_, ws_, rw_, ALU.mult)
                dve.drain()
                nc.vector.tensor_copy(rb[:, ds(blk * BT, BT)], rs_)
                nc.vector.tensor_tensor(rbp[slot], rs_, nn, ALU.mult)
                dve.drain()
                nc.vector.tensor_tensor(rbp[slot], rbp[slot], cc[slot], ALU.add)
                dve.drain()
                nc.vector.tensor_tensor(cc[slot], cc[slot], ws_, ALU.add).then_inc(s_msp, 1)

            def out_tiles(k, slot, some):
                for t in some:
                    zt = z1[:, t * DH:(t + 1) * DH]
                    bank = O[t % 2]
                    n = (k - 1) * BT + t + 1
                    dve.wait_ge(s_o1, n)
                    alone(dve)
                    dve.wait_ge(s_pre, n)
                    alone(dve)
                    nc.vector.tensor_tensor(zt, bank[:, DH:2 * DH], pre[t % 2], ALU.add)
                    dve.drain()
                    nc.vector.scalar_tensor_tensor(zt, bank[:, 0:DH], rbp[slot][:, t:t + 1], zt, ALU.mult, ALU.add).then_inc(s_o1u, 1)
                dve.drain()

            def normalise(k):
                stats(lambda t: z1[:, t * DH:(t + 1) * DH], BT).then_inc(s_mv, 1)
                dve.wait_ge(s_rstd, k)
                alone(dve)
                for t in range(BT):
                    zt = z1[:, t * DH:(t + 1) * DH]
                    last = nc.vector.tensor_scalar(zt, zt, mv8[:, t, 0:1], rstd[:, t:t + 1], ALU.subtract, ALU.mult)
                last.then_inc(s_z, 1)

            def layer2_inputs(k):
                blk = scan(dve, k - 1)
                dve.drain()
                for u in range(2):
                    dve.wait_ge(s_u2, (k - 1) * 2 + u + 1)
                    alone(dve)
                    src = O[u].rearrange("p (t c) -> p t c", t=2, c=2 * D)
                    cols = ds(blk * BW + u * 2 * D, 2 * D)
                    nc.vector.tensor_tensor(tiles(U[:, cols], 2), src[:, :, 0:D], b_us[:, 0:D].unsqueeze(1).to_broadcast([P, 2, D]), ALU.add)
                    nc.vector.tensor_tensor(tiles(R[:, cols], 2), src[:, :, D:2 * D], b_us[:, D:2 * D].unsqueeze(1).to_broadcast([P, 2, D]),
                                            ALU.add).then_inc(s_u2u, 1)

            def collect(k):
                dve.wait_ge(s_agg, k)
                alone(dve)
                dve.wait_ge(s_neh, k)
                alone(dve)

            def step(k, slot, rnd, has):
                n_slot, n_rnd = 1 - slot, rnd + slot
                scales(k, slot)
                if has[-2]:
                    layer2_inputs(k - 1)
                if has[-1]:
                    collect(k)
                    nc.vector.tensor_tensor(aT, PA[1 - slot][:, :], U[:, ds(scan(dve, k - 1) * BW, BW)], ALU.add).then_inc(s_aT, 1)
                if has[1]:
                    partials(k + 1, n_slot, n_rnd, 1)
                    sum_halves()
                if has[-1]:
                    out_tiles(k, n_slot, (0, 1))
                if has[1]:
                    thresholds(k + 1)
                if has[-1]:
                    out_tiles(k, n_slot, (2, 3))
                    normalise(k)
                if has[1]:
                    verdict(k + 1)
                    mask_if_needed(k + 1, n_slot)
                if has[2]:
                    partials(k + 2, slot, rnd + 1, 0)
                if not has[-2] and has[-1]:
                    dve.wait_ge(s_fill, FILLED)

            partials(0, 0, 0, 0)
            dve.wait_ge(s_rstd0, 1)
            for t in range(LN_DVE):
                tile = S[:, t * D:(t + 1) * D]
                last = nc.vector.tensor_scalar(tile, tile, mv0[:, 2 * t:2 * t + 1], rstd0[:, t:t + 1], ALU.subtract, ALU.mult)
            last.then_inc(s_hn, 1)
            partials(0, 0, 0, 1)
            sum_halves()
            dve.wait_ge(s_wts, 16 * len(WEIGHTS))
            nc.vector.tensor_tensor(b_all[:, :], b_all[:, :], t_bs1, ALU.add)
            nc.vector.tensor_tensor(b_us[:, D:2 * D], b_us[:, D:2 * D], t_bs2, ALU.add)
            dve.wait_ge(s_wprod, 1)
            nc.vector.tensor_copy(W_io[:, :], O[0][:, 0:DH])
            nc.vector.tensor_copy(b_io[:, :], O[0][:, DH:2 * DH])
            nc.vector.tensor_copy(W_us[:, :, 0:D], tiles(O[1][:, 0:2 * D], KH))
            nc.vector.tensor_copy(b_us[:, 0:D], O[1][:, 2 * D:3 * D]).then_inc(s_wready, 1)
            thresholds(0)
            verdict(0)
            mask_if_needed(0, 0)
            partials(1, 1, 0, 0)
            peeled1(dve, step)
            layer2_inputs(NB - 1)
            collect(NB)
            nc.vector.tensor_tensor(aT, PA[1][:, :], U[:, 0:BW], ALU.add).then_inc(s_aT, 1)
            out_tiles(NB, 1, range(BT))
            normalise(NB)
            layer2_inputs(NB)
            dve.wait_ge(s_own, NB)
            dve.drain()

            def mask2(j, slot, landed):
                for q in range(4):
                    dve.wait_ge(s_ring[slot][q], landed)
                    alone(dve)
                flag = dve.value_load(flags[0:1, ds(j, 1)], min_val=0, max_val=2 * P)
                with dve.If(flag > 0):
                    mask_block(slot, thr2[slot], msk)
                dve.drain().then_inc(s_clean2, 1)

            def lnorm(k, which, src, dst_of):
                stats(src, BT).then_inc(s_mv2, 1)
                dve.wait_ge(s_rstd2, k * 2 - 1 + which)
                alone(dve)
                for t in range(BT):
                    last = nc.vector.tensor_scalar(dst_of(t), src(t), mv8[:, t, 0:1], rstd[:, t:t + 1],
                                                   ALU.subtract, ALU.mult)
                return last

            def bc3(ap):
                return ap.unsqueeze(1).to_broadcast([P, BT, D])

            def e3(ap):
                return tiles(ap, BT, E1)

            def bce(ap):
                return ap.unsqueeze(2).to_broadcast([P, BT, E1])

            rows3 = tiles(rows, BT, ROW)

            def add_branch(k):
                j = k - 1
                nc.vector.tensor_copy(rb4, rb[:, ds(j * BT, BT)])
                dve.wait_ge(s_t2, k + 1)
                alone(dve)
                dve.drain()
                for t in range(BT):
                    c = slice(t * D, (t + 1) * D)
                    last = nc.vector.scalar_tensor_tensor(o2[:, c], T[0][:, c], rb4[:, t:t + 1], R[:, ds(j * BW + t * D, D)], ALU.mult, ALU.add)
                last.then_inc(s_t2u, 1)
                dve.drain()
                lnorm(k, 0, lambda t: o2[:, t * D:(t + 1) * D], lambda t: o2[:, t * D:(t + 1) * D])
                dve.drain()
                nc.vector.tensor_tensor(tiles(o2), tiles(o2), bc3(g2), ALU.mult)
                dve.drain()
                nc.vector.tensor_tensor(tiles(o2), tiles(o2), bc3(be2), ALU.add)
                dve.drain()
                dve.wait_ge(s_xb, k * 16)
                alone(dve)
                x1 = S[:, ds(j * BW, BW)]
                nc.vector.scalar_tensor_tensor(x1, o2, 0.0, xb, ALU.max, ALU.add).then_inc(s_x1, 1)
                dve.drain()

            def route(k):
                j = k - 1
                if not isinstance(k, int) or k > 1:
                    dve.wait_ge(s_sc, (k - 1) * (16 * BT))
                    alone(dve)
                lnorm(k, 1, lambda t: S[:, ds(j * BW + t * D, D)], lambda t: rows[:, t * ROW:t * ROW + D]).then_inc(s_hn2, 1)
                dve.wait_ge(s_lg, k)
                alone(dve)
                nc.vector.tensor_tensor(lg, SR[:, 0:BT * E1], gbc, ALU.add)
                dve.drain()
                nc.vector.tensor_reduce(lmax, e3(lg), AX.X, ALU.max)
                dve.drain()
                nc.vector.tensor_tensor(e3(lg), e3(lg), bce(lmax), ALU.subtract).then_inc(s_l2, 1)
                dve.wait_ge(s_ex, k)
                alone(dve)
                nc.vector.tensor_reduce(esum, e3(ex), AX.X, ALU.add)
                nc.vector.tensor_reduce(lmax, e3(ex), AX.X, ALU.max)
                dve.drain()
                nc.vector.reciprocal(esum, esum)
                nc.vector.tensor_tensor(e3(sc), e3(ex), bce(lmax), ALU.is_equal)
                dve.drain()
                nc.vector.tensor_tensor(rows3[:, :, D], lmax, esum, ALU.mult)
                nc.vector.tensor_tensor(sc, sc, w8, ALU.mult)
                nc.vector.tensor_copy(rows3[:, :, D + 1], tok)
                dve.drain()
                nc.vector.tensor_reduce(lmax, e3(sc), AX.X, ALU.max)
                nc.vector.tensor_scalar(tok, tok, float(BW), None, ALU.add)
                dve.drain()
                nc.vector.tensor_tensor(e3(oh), e3(sc), bce(lmax), ALU.is_equal).then_inc(s_oh, 1)
                dve.wait_ge(s_cum, k)
                alone(dve)
                for t in range(BT):
                    nc.vector.tensor_tensor(off[:, (t + 1) * E1:(t + 2) * E1], SM[:, (BT + t) * E1:(BT + t + 1) * E1],
                                            off[:, t * E1:(t + 1) * E1], ALU.add)
                    dve.drain()
                nc.vector.tensor_tensor(cw, SM[:, 0:BT * E1], off[:, 0:BT * E1], ALU.add)
                dve.drain()
                nc.vector.tensor_copy(off[:, 0:E1], off[:, BT * E1:(BT + 1) * E1])
                nc.vector.tensor_scalar(sc, cw, float(CAP), NOWHERE, ALU.is_gt, ALU.mult)
                nc.vector.tensor_tensor(cw, cw, cofs, ALU.add)
                dve.drain()
                nc.vector.tensor_tensor(cw, cw, sc, ALU.add)
                dve.drain()
                nc.vector.tensor_tensor(cw, cw, oh, ALU.mult)
                dve.drain()
                nc.vector.tensor_reduce(slot_f, e3(cw), AX.X, ALU.add)
                dve.drain()
                nc.vector.tensor_copy(idx, slot_f).then_inc(s_idx, 1)
                dve.drain()

            dve.wait_ge(s_const, 2)
            dve.wait_ge(s_wts2, 48)
            def step2(k, slot, n_rnd):
                add_branch(k)
                dve.wait_ge(s_thr2[slot], n_rnd * 16)
                alone(dve)
                mask2(k + 1, slot, n_rnd * 16 + 64)
                route(k)

            step2(1, 1, 1)
            with dve.Fori(1, NB // 2 - 1) as i:
                step2(i * 2, 0, i)
                step2(i * 2 + 1, 1, i + 1)
            step2(NB - 2, 0, NB // 2 - 1)
            for k in (NB - 1, NB):
                add_branch(k)
                route(k)

            dve.wait_ge(s_agg2, NB)
            nc.vector.memset(small[:, 4:8], 0.0).then_inc(s_hm, 4)
            nc.vector.memset(small[:, 8:12], 0.0).then_inc(s_out, 1)
            nc.vector.memset(small[:, 12:16], 0.0).then_inc(s_ye, 1)
            nc.vector.memset(small[:, 16:20], 0.0).then_inc(s_oT, 2)
            nc.vector.memset(small[:, 20:24], 0.0).then_inc(s_oTt, 1)
            nc.vector.memset(small[:, 24:28], 0.0).then_inc(s_wu, WS)

            def expert(e, par, rnd):
                er = tiles(e_rows[par], CT, ROW)

                def read(n):
                    lo, hi = EPARTS[n]
                    dve.wait_ge(s_yp, e * 2 + n + 1)
                    alone(dve)
                    return nc.vector.tensor_tensor(tiles(e_y[par][:, lo * D:hi * D], hi - lo), tiles(O[n][:, 0:(hi - lo) * D], hi - lo),
                                                   e_b2[par].unsqueeze(1).to_broadcast([P, hi - lo, D]), ALU.add)

                def scale(n):
                    for q in range(*EPARTS[n]):
                        yq = e_y[par][:, q * D:(q + 1) * D]
                        nc.vector.tensor_scalar(yq, yq, e_prob[par][:, q:q + 1], None, ALU.mult)
                    dve.drain()

                def finite(n):
                    lo, hi = EPARTS[n]
                    y, fin, pos, neg = [v[:, lo * D:hi * D] for v in (e_y[par], e_fin, e_pos, e_neg)]
                    nc.vector.tensor_scalar(fin, y, 0.0, 0.0, ALU.mult, ALU.is_equal)
                    nc.vector.tensor_scalar(pos, y, FMAX, BIG, ALU.is_gt, ALU.mult)
                    nc.vector.tensor_scalar(neg, y, -FMAX, -BIG, ALU.is_lt, ALU.mult)
                    dve.drain()
                    nc.vector.tensor_scalar(y, y, FMAX, -FMAX, ALU.min, ALU.max)
                    dve.drain()
                    nc.vector.tensor_tensor(y, y, fin, ALU.mult)
                    dve.drain()
                    nc.vector.tensor_tensor(y, y, pos, ALU.add)
                    dve.drain()
                    nc.vector.tensor_tensor(y, y, neg, ALU.add).then_inc(s_y, 1)
                    dve.drain()

                dve.wait_ge(s_yp, e * 2 + 1)
                alone(dve)
                if rnd is not None:
                    dve.wait_ge(s_sc2[par], rnd * (16 * CT))
                    alone(dve)
                nc.vector.tensor_copy(e_prob[par], er[:, :, D])
                nc.vector.tensor_copy(e_idx[par], er[:, :, D + 1])
                read(0)
                dve.drain()
                scale(0)
                read(1).then_inc(s_ye, 1)
                finite(0)
                scale(1)
                finite(1)

            expert(0, 0, None)
            expert(1, 1, None)
            with dve.Fori(1, E1 // 2) as i:
                expert(i * 2, 0, i)
                expert(i * 2 + 1, 1, i)

            dve.wait_ge(s_wts3, 16 * len(F2_INPUTS))
            for l in range(L2):
                for kk in range(KH):
                    diag = w_s[:, (l * KH + kk) * DH + kk * P:(l * KH + kk) * DH + (kk + 1) * P]
                    nc.vector.tensor_tensor(diag, diag, ident[:, :], ALU.add)
                    lm = l * KH + kk
                    nc.vector.tensor_scalar(b_r[:, lm * E2:(lm + 1) * E2], b_r[:, lm * E2:(lm + 1) * E2], b_s[:, lm:lm + 1], None, ALU.add)
            dve.drain().then_inc(s_fin2, 1)

            def add_y(c):
                cols = slice(CHUNKS[c][0] * D, CHUNKS[c][1] * D)
                dve.wait_ge(s_yin[c], 16)
                nc.vector.tensor_tensor(R[:, cols], R[:, cols], S[:, cols], ALU.add)

            add_y(0)
            for c, (lo, hi) in enumerate(CHUNKS):
                dve.drain()
                for t in range(lo, hi):
                    nc.vector.bn_stats(st6[:, 6 * (t - lo):6 * (t - lo) + 6], R[:, t * D:(t + 1) * D])
                dve.drain()
                for t in range(lo, hi):
                    last = nc.vector.bn_aggr(mv3[:, 2 * t:2 * t + 2], st6[:, 6 * (t - lo):6 * (t - lo) + 6])
                last.then_inc(s_mv3, 1)
                if hi < NT:
                    add_y(c + 1)
                if c < FIRST:
                    dve.wait_ge(s_rstd3, c + 1)
                    for t in range(lo, hi):
                        tc = slice(t * D, (t + 1) * D)
                        last = nc.vector.tensor_scalar(S[:, tc], R[:, tc], mv3[:, 2 * t:2 * t + 1], rstd3[:, t:t + 1], ALU.subtract, ALU.mult)
                    last.then_inc(s_hid, 1)

            dve.wait_ge(s_ring[0][0], 16 * 8)
            dve.wait_ge(s_ring[0][2], 16 * 8)
            dve.wait_ge(s_ring[0][3], 16 * 8)

            def stage_w(k, l, s):
                n = l * SB + s
                dve.wait_ge(s_wu, (k - 1) * (L2 * SB) + n + 1)
                alone(dve)
                e = dve.value_load(route_sb[0:1, ds((k - 1) * SB + s, 1)], min_val=0, max_val=E2 - 1)
                nc.vector.tensor_tensor(wst[n % WS], ring[0][l][:, ds(e * (KH * DH), KH * DH)],
                                        w_s[:, l * KH * DH:(l + 1) * KH * DH], ALU.add).then_inc(s_wst, 1)

            def step3(k):
                dve.wait_ge(s_oTt, k + 1)
                alone(dve)
                nc.vector.tensor_tensor(x3, T[0][:, :], R[:, ds((k - 1) * BW, BW)], ALU.add).then_inc(s_x3, 1)
                dve.drain()
                stats(lambda t: x3[:, t * D:(t + 1) * D], BT).then_inc(s_mv4, 1)
                for n in range(2):
                    stage_w(k, 0, n)
                dve.wait_ge(s_rstd4, k)
                alone(dve)
                for t in range(BT):
                    c = slice(t * D, (t + 1) * D)
                    last = nc.vector.tensor_scalar(hn3[:, c], x3[:, c], mv8[:, t, 0:1], rstd[:, t:t + 1], ALU.subtract, ALU.mult)
                last.then_inc(s_hn3, 1)
                for n in range(2, L2 * SB):
                    stage_w(k, n // SB, n % SB)
                dve.wait_ge(s_fin, k)
                alone(dve)
                dve.wait_ge(s_x3b, k)
                alone(dve)
                if not isinstance(k, int) or k > 1:
                    dve.wait_ge(s_stored, (k - 1) * 16)
                    alone(dve)
                nc.vector.tensor_tensor(ob, T[0][:, :], x3, ALU.add).then_inc(s_out, 1)
                dve.drain()

            step3(1)
            with dve.Fori(1, NB // 2) as i:
                step3(i * 2)
                step3(i * 2 + 1)
            step3(NB)

        @block.tensor
        def _(pe):
            pe.wait_ge(s_wts, 16 * len(WEIGHTS))
            pe.wait_ge(s_const, 1)
            for kk in range(KH):
                nc.tensor.matmul(O[0][:, 0:DH], t_in1T[:, kk * P:(kk + 1) * P], t_out1[:, kk * DH:(kk + 1) * DH], start=kk == 0, stop=kk == KH - 1)
            for kk in range(KH):
                nc.tensor.matmul(O[0][:, DH:2 * DH], t_bin1[:, kk * P:(kk + 1) * P], t_out1[:, kk * DH:(kk + 1) * DH], start=kk == 0, stop=kk == KH - 1)
            for kk in range(KH):
                nc.tensor.matmul(O[1][:, kk * D:(kk + 1) * D], t_in2T[:, kk * P:(kk + 1) * P], t_out2, start=True, stop=True)
            nc.tensor.matmul(O[1][:, 2 * D:3 * D], t_bin2, t_out2, start=True, stop=True).then_inc(s_wprod, 1)

            def keep_warm(n, moving, bank):
                for _ in range(n):
                    nc.tensor.matmul(bank[:, :], ident[:, :], moving, start=True, stop=True)

            keep_warm(1, t_out1, PA[0])

            def sums(cols, s):
                nc.tensor.matmul(SR[:, :], ones[:, :], pA, start=True, stop=True)
                for t in range(BT):
                    last = nc.tensor.matmul(SM[:, cols + t:cols + t + 1], pA[:, t * P:(t + 1) * P], ones[:, 0:1], start=True, stop=True)
                last.then_inc(s, 1)

            def raw_sums(k, first=False):
                pe.wait_ge(s_part, k + 1)
                if not first:
                    pe.wait_ge(s_msp, k)
                sums(0, s_sums)

            def sum_verdict(k):
                pe.wait_ge(s_bad, k + 2)
                nc.tensor.matmul(SM[0:1, 2 * BT:2 * BT + 1], bad, ones[:, 0:1], start=True, stop=True).then_inc(s_flag, 1)

            def products(X, slot, lo, hi, s_quarter, order=range(NT), bank=None):
                out_T = PA[slot if bank is None else bank]
                for n in range(lo, hi):
                    t = order[n]
                    mm = nc.tensor.matmul(out_T[:, :], X[:, t * D:(t + 1) * D], ring[slot][t // HT][:, (t % HT) * BW:(t % HT + 1) * BW],
                                          start=n == 0, stop=n == NT - 1)
                    if n % QT == QT - 1 and n < NT - 1:
                        mm.then_inc(s_quarter, 1)
                return mm

            def out_rows(k, tiles_of_block):
                pe.wait_ge(s_wready, 1)
                pe.wait_ge(s_aT, k + 2)
                for t in tiles_of_block:
                    if t < 2:
                        pe.wait_ge(s_u2u, (k - 1) * 2 + t + 1)
                    else:
                        pe.wait_ge(s_o1u, (k - 1) * BT + t + 1)
                    nc.tensor.matmul(O[t % 2][:, 0:DH], aT[:, t * P:(t + 1) * P], W_io[:, :], start=True, stop=True)
                    nc.tensor.matmul(O[t % 2][:, DH:2 * DH], hT[:, t * P:(t + 1) * P], W_s1[:, :], start=True, stop=True).then_inc(s_o1, 1)

            def turn_h(k):
                pe.wait_ge(s_hs, k + 1)
                for t in range(BT):
                    last = nc.tensor.transpose(T[0][:, t * P:(t + 1) * P], hs[:, t * P:(t + 1) * P], ident[:, :])
                last.then_inc(s_hTp, 1)

            def turn_z(k):
                pe.wait_ge(s_z, k)
                for f in range(KH):
                    for t in range(BT):
                        last = nc.tensor.transpose(T[f][:, t * P:(t + 1) * P], z1[:, t * DH + f * P:t * DH + (f + 1) * P], ident[:, :])
                last.then_inc(s_zT, 1)

            def layer2_products(k):
                pe.wait_ge(s_h1T, k)
                for t in range(BT):
                    if t % 2 == 0:
                        pe.wait_ge(s_o1u, (k - 1) * BT + t // 2 + 5)
                    o = O[t // 2][:, (t % 2) * 2 * D:(t % 2 + 1) * 2 * D]
                    for f in range(KH):
                        mm = nc.tensor.matmul(o, h1T[:, f * BW + t * P:f * BW + (t + 1) * P], W_us[:, f, :], start=f == 0, stop=f == KH - 1)
                    if t % 2 == 1:
                        mm.then_inc(s_u2, 1)

            def step(k, slot, rnd, has):
                pe.wait_ge(s_clean, k + 1)
                sums(BT, s_ms)
                pe.wait_ge(s_aT, k + 1)
                products(S, slot, 0, 12, s_quart)
                if has[-1]:
                    out_rows(k, (0, 1))
                products(S, slot, 12, 20, s_quart)
                if has[1]:
                    raw_sums(k + 1)
                products(S, slot, 20, 23, s_quart)
                if has[-1]:
                    out_rows(k, (2, 3))
                products(S, slot, 23, 30, s_quart)
                if has[-1]:
                    pe.wait_ge(s_hT, k)
                    turn_z(k)
                products(S, slot, 30, 31, s_quart)
                if has[1]:
                    sum_verdict(k + 1)
                products(S, slot, 31, NT, s_quart).then_inc(s_agg, 1)
                if has[-1]:
                    layer2_products(k)
                turn_h(k)

            raw_sums(0, True)
            sum_verdict(0)
            pe.wait_ge(s_hn, 2)
            peeled1(pe, step)

            def tail_a(k):
                pe.wait_ge(s_p2, k + 2)
                pe.wait_ge(s_t2u, k)
                for t in range(BT):
                    last = nc.tensor.transpose(T[0][:, t * P:(t + 1) * P], p2T[:, t * P:(t + 1) * P], ident[:, :])
                last.then_inc(s_t2, 1)

            def tail_b(k):
                pe.wait_ge(s_hn2, k)
                for t in range(BT):
                    last = nc.tensor.transpose(T[1][:, t * P:(t + 1) * P], rows[:, t * ROW:t * ROW + D], ident[:, :])
                last.then_inc(s_hn2p, 1)

            def tail_c(k):
                pe.wait_ge(s_hn2T, k)
                for t in range(BT):
                    last = nc.tensor.matmul(SR[:, t * E1:(t + 1) * E1], hnT[:, t * P:(t + 1) * P], wgate[:, :], start=True, stop=True)
                last.then_inc(s_lg, 1)

            def tail_d(k):
                pe.wait_ge(s_oh, k)
                nc.tensor.matmul(SM[:, 0:BT * E1], tri[:, :], oh, start=True, stop=True)
                nc.tensor.matmul(SM[:, BT * E1:2 * BT * E1], onesb[:, :], oh, start=True, stop=True).then_inc(s_cum, 1)

            def step2(k, slot, rnd, prev, nxt):
                sl = 1 - slot
                if not prev:
                    products(U, sl, 0, 4, s_quart2, ROWS2, slot)
                    out_rows(NB, (0, 1))
                    products(U, sl, 4, 9, s_quart2, ROWS2, slot)
                    out_rows(NB, (2, 3))
                    products(U, sl, 9, 18, s_quart2, ROWS2, slot)
                    turn_z(NB)
                    products(U, sl, 18, 21, s_quart2, ROWS2, slot)
                    layer2_products(NB)
                    products(U, sl, 21, NT - BT, s_quart2, ROWS2, slot)
                    pe.wait_ge(s_u2u, 2 * NB + 2)
                    products(U, sl, NT - BT, NT, s_quart2, ROWS2, slot).then_inc(s_agg2, 1)
                    return
                pe.wait_ge(s_clean2, k + 1)
                pe.wait_ge(s_p2, k + 1)
                products(U, sl, 0, 2, s_quart2, ROWS2, slot)
                tail_a(k)
                products(U, sl, 2, 20, s_quart2, ROWS2, slot)
                tail_b(k)
                products(U, sl, 20, 23, s_quart2, ROWS2, slot)
                tail_c(k)
                products(U, sl, 23, 28, s_quart2, ROWS2, slot)
                tail_d(k)
                products(U, sl, 28, NT, s_quart2, ROWS2, slot).then_inc(s_agg2, 1)

            def last2(k):
                tail_a(k)
                tail_b(k)
                tail_c(k)
                tail_d(k)

            peeled(pe, step2, last2)

            def turn_rows(par, rnd):
                pe.wait_ge(s_rin[par], rnd * 16 + 16)
                xr = e_rows[par]
                for q in range(CT):
                    bank, c = (T[0], q) if q < BT else (T[1], 0)
                    last = nc.tensor.transpose(bank[:, c * P:(c + 1) * P], xr[:, q * ROW:q * ROW + D], ident[:, :])
                last.then_inc(s_xTp, 1)

            def expert(e, par, rnd, more):
                pe.wait_ge(s_ein[par], rnd * 64 + 64)
                pe.wait_ge(s_xT, e + 1)
                for q in range(2 * FK):
                    f, c = q // 2, q % 2
                    pe.wait_ge(s_hm, e * (2 * FK) + q + 1)
                    nc.tensor.matmul(HB[q % 4][:, 0:CAP // 2], e_w1[par][:, f * P:(f + 1) * P], e_xT[:, c * CAP // 2:(c + 1) * CAP // 2],
                                     start=True, stop=True).then_inc(s_h1, 1)
                if more:
                    turn_rows(1 - par, rnd + par)
                pe.wait_ge(s_hm, e * (2 * FK) + 2 * FK + 4)
                pe.wait_ge(s_ye, e + 1)
                for bank, (lo, hi) in zip(O, EPARTS):
                    for q in range(lo, hi):
                        c = q - lo
                        for f in range(FK):
                            mm = nc.tensor.matmul(bank[:, c * D:(c + 1) * D], e_hm[:, f * CAP + q * P:f * CAP + (q + 1) * P],
                                                  e_w2[par][:, f * D:(f + 1) * D], start=f == 0, stop=f == FK - 1)
                    mm.then_inc(s_yp, 1)

            pe.wait_ge(s_idx, NB)
            keep_warm(7, S[:, 0:BW], PA[0])
            turn_rows(0, 0)
            with pe.Fori(0, E1 // 2 - 1) as i:
                expert(i * 2, 0, i, True)
                expert(i * 2 + 1, 1, i, True)
            expert(E1 - 2, 0, E1 // 2 - 1, True)
            expert(E1 - 1, 1, E1 // 2 - 1, False)

            pe.wait_ge(s_yin[0], 16)
            keep_warm(3, e_w1[0], PA[0])

            def products3(k, slot, lo, hi):
                for t in range(lo, hi):
                    for c, (first, _) in enumerate(CHUNKS):
                        if t == first and isinstance(k, int) and k == 0:
                            if c < FIRST:
                                pe.wait_ge(s_hid, c + 1)
                            else:
                                pe.wait_ge(s_hid2, c + 1 - FIRST)
                    if t % QT == 0:
                        pe.wait_ge(s_ring[1][t // QT], k * 16 + 128)
                    mm = nc.tensor.matmul(PA[slot][:, :], S[:, t * D:(t + 1) * D], ring[1][t // HT][:, (t % HT) * BW:(t % HT + 1) * BW],
                                          start=t == 0, stop=t == NT - 1)
                    if t % QT == QT - 1 and t < NT - 1:
                        mm.then_inc(s_quart3, 1)
                return mm

            def turn_sum(k):
                pe.wait_ge(s_oT, k + 2)
                pe.wait_ge(s_out, k)
                for t in range(BT):
                    last = nc.tensor.transpose(T[0][:, t * P:(t + 1) * P], oT[:, t * P:(t + 1) * P], ident[:, :])
                last.then_inc(s_oTt, 1)

            def turn_hn3(k):
                pe.wait_ge(s_hn3, k)
                for t in range(BT):
                    last = nc.tensor.transpose(T[1][:, t * P:(t + 1) * P], hn3[:, t * P:(t + 1) * P], ident[:, :])
                last.then_inc(s_hn3p, 1)

            def h0(k):
                pe.wait_ge(s_hT3, k)
                for m in range(KH):
                    last = nc.tensor.matmul(O[m][:, :], w_i[:, m * P:(m + 1) * P], hT3, start=True, stop=True)
                last.then_inc(s_h0p, 1)

            def routed(k, g):
                l, half = g * SH // SB, g % (SB // SH)
                src = (h_a, h_b)[l]
                if g == 0:
                    pe.wait_ge(s_h0, k)
                if l == 1:
                    pe.wait_ge(s_l, (k - 1) * NG + g - SB // SH + 1)
                for s in range(half * SH, (half + 1) * SH):
                    n = l * SB + s
                    pe.wait_ge(s_wst, (k - 1) * (L2 * SB) + n + 1)
                    for m in range(KH):
                        at = m * SH * SEG + s % SH * SEG
                        for kk in range(KH):
                            mm = nc.tensor.matmul(LB[g][:, at:at + SEG], wst[n % WS][:, kk * DH + m * P:kk * DH + (m + 1) * P],
                                                  src[:, kk * BW + s * SEG:kk * BW + (s + 1) * SEG], start=kk == 0, stop=kk == KH - 1)
                    mm.then_inc(s_wu, 1)

            def out_proj(k):
                pe.wait_ge(s_l, k * NG)
                for t in range(BT):
                    for kk in range(KH):
                        mm = nc.tensor.matmul(T[0][:, t * D:(t + 1) * D], h_a[:, kk * BW + t * P:kk * BW + (t + 1) * P],
                                              w_o[:, kk * D:(kk + 1) * D], start=kk == 0, stop=kk == KH - 1)
                mm.then_inc(s_fin, 1)

            TAIL3 = [(2, turn_sum), (10, turn_hn3), (12, h0), (14, lambda k: routed(k, 0)), (18, lambda k: routed(k, 1)),
                     (22, lambda k: routed(k, 2)), (26, lambda k: routed(k, 3)), (31, out_proj), (NT, None)]

            def step3(k, slot, rnd, prev, nxt):
                pe.wait_ge(s_oT, k + 1)
                done = 0
                for n, piece in TAIL3:
                    if n > done:
                        mm = products3(k, slot, done, n)
                    if n == NT:
                        mm.then_inc(s_agg3, 1)
                    if prev and piece:
                        piece(k)
                    done = n

            def last3(k):
                for (n, piece), idle in zip(TAIL3[:-1], (0, 6, 1, 1, 0, 0, 0, 4)):
                    keep_warm(idle, S[:, 0:BW], PA[0])
                    piece(k)

            peeled(pe, step3, last3)


def kernel(**inputs):
    import numpy as _np
    import concourse.bacc as _bacc
    from concourse import mybir as _mybir
    from concourse.bass_utils import run_bass_kernel_spmd as _run

    g = {k: _np.asarray(v) for k, v in inputs.items()}

    def cols(M):
        return M.reshape(NT, P, NB, BW).transpose(2, 1, 0, 3).reshape(NB, P, NT * BW)

    def bc(v):
        return _np.broadcast_to(v.reshape(1, -1), (P, v.size))

    def by_part(W):
        return W.reshape(-1, P, W.shape[1]).transpose(1, 0, 2)

    def rep(v):
        return _np.broadcast_to(v.reshape(-1, P).T[:, :, None], (P, v.size // P, P)).reshape(P, -1)

    L = {
        "x": g["x"],
        "adj_cols": cols(g["adj"]),
        "adjT_cols": cols(g["adj"].T),
        "W_in1T": by_part(_np.ascontiguousarray(g["L0_gnn_W_in1"].T)).reshape(P, -1),
        "W_out1": by_part(g["L0_gnn_W_out1"]).reshape(P, -1),
        "W_in2T": g["L0_gnn_W_in2"].T,
        "W_out2": g["L0_gnn_W_out2"],
        "b_in1_rep": rep(g["L0_gnn_b_in1"]),
        "b_in2_rep": rep(g["L0_gnn_b_in2"]),
        "b_self1_bc": bc(g["L0_gnn_b_self1"]),
        "b_self2_bc": bc(g["L0_gnn_b_self2"]),
        "b_out1_bc": bc(g["L0_gnn_b_out1"]),
        "b_out2_bc": bc(g["L0_gnn_b_out2"]),
        "W_self1": g["L0_gnn_W_self1"],
        "W_self2": by_part(g["L0_gnn_W_self2"]),
        "gb1": _np.concatenate([g["L0_gnn_g1"].reshape(KH, P).T, g["L0_gnn_be1"].reshape(KH, P).T], axis=1),
        "gate_w": g["L0_ffn_gate_w"],
        "g2_bc": bc(g["L0_gnn_g2"]),
        "be2_bc": bc(g["L0_gnn_be2"]),
        "gate_b_bc": _np.tile(bc(g["L0_ffn_gate_b"]), (1, BT)),
        "w1": g["L0_ffn_w1"],
        "w2": g["L0_ffn_w2"].reshape(E1, FK, P, D).transpose(0, 2, 1, 3).reshape(E1, P, FK * D),
        "b1": g["L0_ffn_b1"].reshape(E1, FK, P).transpose(0, 2, 1),
        "b2_bc": _np.broadcast_to(g["L0_ffn_b2"][:, None, :], (E1, P, D)),
        "gnn_W": g["L1_gnn_W"].reshape(P, 1),
        "route": g["L1_ffn_route_id"].reshape(1, -1),
        "WiT": g["L1_ffn_Wi"].T,
        "bi": g["L1_ffn_bi"].reshape(KH, P).T,
        "Wr": g["L1_ffn_Wr"].reshape(L2, E2, DH, KH, P).transpose(0, 4, 1, 3, 2).reshape(L2, P, E2 * KH * DH),
        "br": g["L1_ffn_br"].reshape(L2, E2, KH, P).transpose(3, 0, 2, 1).reshape(P, L2 * KH * E2),
        "WsT": g["L1_ffn_Ws"].reshape(L2, DH, KH, P).transpose(3, 0, 2, 1).reshape(P, L2 * KH * DH),
        "bs": g["L1_ffn_bs"].reshape(L2, KH, P).transpose(2, 0, 1).reshape(P, L2 * KH),
        "WoT": by_part(_np.ascontiguousarray(g["L1_ffn_Wo"].T)).reshape(P, -1),
        "bo_bc": bc(g["L1_ffn_bo"]),
    }
    nc = _bacc.Bacc("TRN2", target_bir_lowering=False, num_devices=1)
    arrays, A = {}, {}
    for name, a in L.items():
        a = _np.ascontiguousarray(a)
        arrays[f"in_{name}"] = a
        A[name] = nc.dram_tensor(f"in_{name}", a.shape, _mybir.dt.from_np(a.dtype), kind="ExternalInput").ap()
    out = nc.dram_tensor("out_x", (N, D), F32, kind="ExternalOutput").ap()
    build(nc, A, out)
    r = _run(nc, [arrays], core_ids=[0])
    return r.results[0]["out_x"]
```
